# Optimizing a Trainium2 kernel written in Bass

```python
import numpy as np
import jax
import jax.numpy as jnp

def _softmax(x, axis=-1):
    return jax.nn.softmax(x, axis=axis)

def _gelu(x):
    return jax.nn.gelu(x, approximate=True)

def _silu(x):
    return jax.nn.silu(x)

def _sigmoid(x):
    return jax.nn.sigmoid(x)

def _layernorm(x, axis=-1, eps=1e-05):
    m = jnp.mean(x, axis=axis, keepdims=True)
    v = jnp.var(x, axis=axis, keepdims=True)
    return (x - m) / jnp.sqrt(v + eps)

def _scatter_add(tgt, idx, src, axis=0):
    return tgt.at[idx].add(src)

def _segment_sum(src, seg, n):
    return jax.ops.segment_sum(src, seg, n)
kernel_name = 'mk_adaln_ffn_d2_seqx_r2_a3fd0e'

def setup_inputs(seed: int=0):
    np.random.seed(seed)
    _w = jnp.asarray

    def _rec_inputs():
        import jax
        import jax.numpy as jnp
        _rk = jax.random.key(seed)
        x = -0.000125 + 0.9999 * jax.random.normal(jax.random.fold_in(_rk, 1), (32, 128, 2048), jnp.float32)
        _lenS = 128 - jax.random.randint(jax.random.fold_in(_rk, 7), (32,), 0, max(1, 128 // 4) + 1, jnp.int32)
        _lenS2 = 128 - jax.random.randint(jax.random.fold_in(_rk, 8), (32,), 0, max(1, 128 // 4) + 1, jnp.int32)
        itok_B_3_7 = jax.random.randint(jax.random.fold_in(_rk, 11), (32,), 3, 8, jnp.int32)
        itok_B_0_7 = jax.random.randint(jax.random.fold_in(_rk, 12), (32,), 0, 8, jnp.int32)
        itok_B_2182_4065 = jax.random.randint(jax.random.fold_in(_rk, 14), (32,), 1091, 2033, jnp.int32)
        return (x, itok_B_3_7, itok_B_0_7, itok_B_2182_4065, _lenS)
    x, itok_B_3_7, itok_B_0_7, itok_B_2182_4065, _lenS = _rec_inputs()

    def _L0_cond_setup():
        import jax, jax.numpy as jnp
        import numpy as np
        RANK = 16
        ALPHA = 16.0
        SCALING = ALPHA / RANK
        N_ADAPTERS = 8
        IN_F = 2048
        OUT_F = 2048
        BATCH = 4
        SEQ = 1024
        key = jax.random.key(seed)
        kx, ka, kb, ki = jax.random.split(key, 4)
        x = jax.random.normal(kx, (BATCH, SEQ, IN_F), dtype=jnp.float32)
        A = jax.random.normal(ka, (N_ADAPTERS, OUT_F, RANK), dtype=jnp.float32) * 0.02
        B = jax.random.normal(kb, (N_ADAPTERS, RANK, IN_F), dtype=jnp.float32) * 0.02
        adapter_ids = jax.random.randint(ki, (BATCH,), 0, N_ADAPTERS, dtype=jnp.int32)
        return {'x': x, 'A': A, 'B': B, 'adapter_ids': adapter_ids}
    _L0_cond_all = _L0_cond_setup()
    _L0_cond_in = {k: v for k, v in _L0_cond_all.items() if k in ('A', 'B')}
    del _L0_cond_all

    def _L0_ffn_setup():
        import jax, jax.numpy as jnp
        import numpy as np
        B, L, H, Dh, M = (4, 1024, 16, 128, 512)
        D = H * Dh
        key = jax.random.key(seed)
        kx, ku, kd, kp = jax.random.split(key, 4)
        x = jax.random.normal(kx, (B, L, D), dtype=jnp.float32)
        up = jax.random.normal(ku, (H, Dh, M), dtype=jnp.float32)
        down = jax.random.normal(kd, (H, M, Dh), dtype=jnp.float32)
        perm = jax.random.permutation(kp, D)
        return {'x': x, 'up': up, 'down': down, 'perm': perm}
    _L0_ffn_all = _L0_ffn_setup()
    _L0_ffn_in = {k: v for k, v in _L0_ffn_all.items() if k in ('up', 'down', 'perm')}
    del _L0_ffn_all

    def _L1_cond_setup():
        import jax, jax.numpy as jnp
        import numpy as np
        SESSION_CHANNELS = [128, 160, 192, 224, 240, 248, 252, 128]
        N_SESS = len(SESSION_CHANNELS)
        B, MAX_C, MAX_T = (16, 128, 2048)
        HID, N_SRC = (256, 128)
        key = jax.random.key(seed)
        ks = jax.random.split(key, 7)
        session_ids = jax.random.randint(ks[0], (B,), 0, N_SESS)
        chan_table = jnp.asarray(SESSION_CHANNELS)
        channel_counts = chan_table[session_ids]
        seq_lens = jax.random.randint(ks[1], (B,), MAX_T // 2, MAX_T + 1)
        x = jax.random.normal(ks[2], (B, MAX_C, MAX_T), jnp.float32)
        cmask = (jnp.arange(MAX_C)[None, :] < channel_counts[:, None]).astype(x.dtype)
        tmask = (jnp.arange(MAX_T)[None, :] < seq_lens[:, None]).astype(x.dtype)
        x = x * cmask[:, :, None] * tmask[:, None, :]
        lim1 = 1.0 / np.sqrt(MAX_C)
        W_sess = jax.random.uniform(ks[3], (N_SESS, MAX_C, HID), jnp.float32, -lim1, lim1)
        b_sess = jax.random.uniform(ks[4], (N_SESS, HID), jnp.float32, -lim1, lim1)
        lim2 = 1.0 / np.sqrt(HID)
        W2 = jax.random.uniform(ks[5], (HID, N_SRC), jnp.float32, -lim2, lim2)
        b2 = jax.random.uniform(ks[6], (N_SRC,), jnp.float32, -lim2, lim2)
        return dict(x=x, session_ids=session_ids, channel_counts=channel_counts, seq_lens=seq_lens, W_sess=W_sess, b_sess=b_sess, W2=W2, b2=b2)
    _L1_cond_all = _L1_cond_setup()
    _L1_cond_in = {k: v for k, v in _L1_cond_all.items() if k in ('W_sess', 'b_sess', 'W2', 'b2')}
    del _L1_cond_all

    def _L1_ffn_setup():
        import jax, jax.numpy as jnp
        import numpy as np
        IN_FEATURES = 2048

        def _dequantize(qweight, scale, zero_point):
            N, K_packed = qweight.shape
            groups = K_packed // 3
            p = qweight.reshape(N, groups, 3)
            v0 = p[:, :, 0] & 63
            v1 = p[:, :, 0] >> 6 & 63
            v2 = p[:, :, 1] & 63
            v3 = p[:, :, 2] & 63
            unpacked = jnp.stack([v0, v1, v2, v3], axis=2).reshape(N, groups * 4)
            unpacked = unpacked[:, :IN_FEATURES]
            return (unpacked.astype(jnp.float32) - zero_point) * scale
        key = jax.random.key(seed)
        k1, k2, k3, k4, k5 = jax.random.split(key, 5)
        x = jax.random.normal(k1, (8, 1024, 2048), dtype=jnp.float32)
        qweight = jax.random.randint(k2, (2048, 1536), 0, 2048, dtype=jnp.int32)
        weight_scale = jax.random.uniform(k3, (2048, 1), dtype=jnp.float32) * 0.02 + 0.001
        weight_zero_point = jax.random.uniform(k4, (2048, 1), dtype=jnp.float32) * 63.0
        bias = jax.random.normal(k5, (2048,), dtype=jnp.float32)
        return {'x': x, 'qweight': qweight, 'weight_scale': weight_scale, 'weight_zero_point': weight_zero_point, 'bias': bias}
    _L1_ffn_all = _L1_ffn_setup()
    _L1_ffn_in = {k: v for k, v in _L1_ffn_all.items() if k in ('qweight', 'weight_scale', 'weight_zero_point', 'bias')}
    del _L1_ffn_all
    return {'x': x, 'itok_B_3_7': itok_B_3_7, 'itok_B_0_7': itok_B_0_7, 'itok_B_2182_4065': itok_B_2182_4065, '_lenS': _lenS, 'L0_cond_A': _L0_cond_in['A'], 'L0_cond_B': _L0_cond_in['B'], 'L0_ffn_up': _L0_ffn_in['up'], 'L0_ffn_down': _L0_ffn_in['down'], 'L0_ffn_perm': _L0_ffn_in['perm'], 'L1_cond_W_sess': _L1_cond_in['W_sess'], 'L1_cond_b_sess': _L1_cond_in['b_sess'], 'L1_cond_W2': _L1_cond_in['W2'], 'L1_cond_b2': _L1_cond_in['b2'], 'L1_ffn_qweight': _L1_ffn_in['qweight'], 'L1_ffn_weight_scale': _L1_ffn_in['weight_scale'], 'L1_ffn_weight_zero_point': _L1_ffn_in['weight_zero_point'], 'L1_ffn_bias': _L1_ffn_in['bias']}

def reference(x, itok_B_3_7, itok_B_0_7, itok_B_2182_4065, _lenS, L0_cond_A, L0_cond_B, L0_ffn_up, L0_ffn_down, L0_ffn_perm, L1_cond_W_sess, L1_cond_b_sess, L1_cond_W2, L1_cond_b2, L1_ffn_qweight, L1_ffn_weight_scale, L1_ffn_weight_zero_point, L1_ffn_bias):
    import jax
    import jax.numpy as jnp

    def _L0_cond_ref(x, A, B, adapter_ids):
        import jax, jax.numpy as jnp
        import numpy as np
        RANK = 16
        ALPHA = 16.0
        SCALING = ALPHA / RANK
        N_ADAPTERS = 8
        IN_F = 2048
        OUT_F = 2048
        BATCH = 4
        SEQ = 1024
        B_sel = B[adapter_ids]
        A_sel = A[adapter_ids]
        Bx = jnp.einsum('bni,bri->bnr', x, B_sel)
        out = jnp.einsum('bnr,bor->bno', Bx, A_sel)
        return out * SCALING

    def _L0_ffn_ref(x, up, down, perm):
        import jax, jax.numpy as jnp
        import numpy as np
        B, L, H, Dh, M = (4, 1024, 16, 128, 512)
        D = H * Dh
        b, l, Dm = x.shape
        h, d = (up.shape[0], up.shape[1])
        unperm = jnp.argsort(perm)
        t = x.reshape(b * l, Dm)
        t = t[:, perm]
        t = t.reshape(b * l, h, d)
        t = jnp.einsum('bhd,hdm->bhm', t, up)
        t = jax.nn.gelu(t, approximate=False)
        t = jnp.einsum('bhm,hmd->bhd', t, down)
        t = t.reshape(b * l, h * d)
        t = t[:, unperm]
        out = t.reshape(b, l, Dm)
        return out

    def _L1_cond_ref(x, session_ids, channel_counts, seq_lens, W_sess, b_sess, W2, b2):
        import jax, jax.numpy as jnp
        import numpy as np
        SESSION_CHANNELS = [128, 160, 192, 224, 240, 248, 252, 128]
        N_SESS = len(SESSION_CHANNELS)
        B, MAX_C, MAX_T = (16, 128, 2048)
        HID, N_SRC = (256, 128)
        cmask = (jnp.arange(x.shape[1])[None, :] < channel_counts[:, None]).astype(x.dtype)
        xm = x * cmask[:, :, None]
        W = W_sess[session_ids]
        b = b_sess[session_ids]
        h = jnp.einsum('bct,bch->bht', xm, W) + b[:, :, None]
        h = jax.nn.gelu(h, approximate=False)
        out = jnp.einsum('bht,hs->bst', h, W2) + b2[None, :, None]
        tmask = (jnp.arange(x.shape[2])[None, :] < seq_lens[:, None]).astype(x.dtype)
        return out * tmask[:, None, :]

    def _L1_ffn_ref(x, qweight, weight_scale, weight_zero_point, bias):
        import jax, jax.numpy as jnp
        import numpy as np
        IN_FEATURES = 2048

        def _dequantize(qweight, scale, zero_point):
            N, K_packed = qweight.shape
            groups = K_packed // 3
            p = qweight.reshape(N, groups, 3)
            v0 = p[:, :, 0] & 63
            v1 = p[:, :, 0] >> 6 & 63
            v2 = p[:, :, 1] & 63
            v3 = p[:, :, 2] & 63
            unpacked = jnp.stack([v0, v1, v2, v3], axis=2).reshape(N, groups * 4)
            unpacked = unpacked[:, :IN_FEATURES]
            return (unpacked.astype(jnp.float32) - zero_point) * scale
        w = _dequantize(qweight, weight_scale, weight_zero_point)
        return jnp.einsum('bsk,nk->bsn', x, w) + bias
    x = x + _L0_ffn_ref(_L0_cond_ref(x, L0_cond_A, L0_cond_B, itok_B_3_7), L0_ffn_up, L0_ffn_down, L0_ffn_perm)
    x = x + _L1_ffn_ref(_L1_cond_ref(x, itok_B_0_7, _lenS, itok_B_2182_4065, L1_cond_W_sess, L1_cond_b_sess, L1_cond_W2, L1_cond_b2), L1_ffn_qweight, L1_ffn_weight_scale, L1_ffn_weight_zero_point, L1_ffn_bias)
    return x

_drawn_inputs = setup_inputs


def setup_inputs(seed=0):
    import zlib

    import numpy as np

    out = dict(_drawn_inputs(seed))
    spreads = {}
    factors = {'L1_cond_b_sess': 5.902, 'L1_ffn_bias': 32.038}
    for name, (base, spread) in spreads.items():
        noise = np.random.default_rng([zlib.crc32(name.encode()), seed]).standard_normal(out[name].shape)
        drawn = base * np.exp(spread * noise) if base else spread * noise
        out[name] = jnp.asarray(drawn.astype(out[name].dtype))
    for name, factor in factors.items():
        out[name] = (out[name] * factor).astype(out[name].dtype)
    return out
```

```python
from contextlib import ExitStack

import numpy as np

import concourse.bass as bass
from concourse import mybir

F32 = mybir.dt.float32
F32R = mybir.dt.float32r
BF16 = mybir.dt.bfloat16
I32 = mybir.dt.int32
ALU = mybir.AluOpType
ACT = mybir.ActivationFunctionType

P = 128
B, C, D = 32, 128, 2048
NA, R = 8, 16
H, M = 16, 512
NS, HID = 8, 256
NK = D // P
GB = 4
GT = GB * C
NG = B // GB
HQ = 4
NQ = H // HQ
MT = M // P
KG = 7 * R
NIT = NQ * NG
STEPS = NIT * HQ
UNROLL = 8
LAST = STEPS // UNROLL
CREDIT = 1


def earlier(i, k, lag):
    i2, k2 = i + (k - lag) // UNROLL, (k - lag) % UNROLL
    if isinstance(i, int) and not 0 <= i2 < LAST:
        return None
    return i2, k2


def step_loop(engine, body, tail):
    for k in range(UNROLL):
        body(0, k)
    with engine.Fori(1, LAST) as i:
        for k in range(UNROLL):
            body(i, k)
    for k in range(tail):
        body(LAST, k)


def wait(engine, sem, count):
    if not (isinstance(count, int) and count <= 0):
        engine.wait_ge(sem, count)


def build(nc, xT, adown, bdown, up, down, w_sess, b_sess, w2, b2, qw, dense, perm, perm_row,
          adapter, session, chan_len, time_len, ident, expand, rows, out):
    with ExitStack() as top:
        def sem(name):
            return top.enter_context(nc.semaphore(name))

        def sb(ctx, name, shape, dt):
            return ctx.enter_context(nc.sbuf_tensor(name, shape, dt))

        g_dram = nc.dram_tensor("g_parts", [NQ * NA, KG, HQ * M], BF16).ap()
        bx_dram = nc.dram_tensor("bx_parts", [NG, P, GT], BF16).ap()
        ws_dram = nc.dram_tensor("ws_parts", [B, P, 2 * HID], F32).ap()
        dw_dram = nc.dram_tensor("down_parts", [H, P, 2 * MT * P], F32).ap()
        y_dram = nc.dram_tensor("y_rows", [NIT, P, HQ, GT], F32).ap()
        x1_dram = nc.dram_tensor("x1_rows", [NG * D, GT], F32).ap()

        ident_sb = sb(top, "ident_sb", [P, P], F32)
        rows_sb = sb(top, "rows_sb", [P, 2], F32)
        perm_sb = sb(top, "perm_sb", [P, NK], I32)
        shift = sb(top, "shift", [P, NK], I32)
        ysum = sb(top, "ysum", [P, STEPS], F32)
        dense_sb = sb(top, "dense_sb", [P, 3, NK], F32)
        nzero = sb(top, "nzero", [P, NK], F32)

        st01 = ExitStack()
        row_idx = sb(st01, "row_idx", [P, NIT, HQ], I32)
        g_idx = sb(st01, "g_idx", [P, NQ, B], I32)
        time_f = sb(st01, "time_f", [P, B], F32)
        permrow_f = sb(st01, "permrow_f", [P, D], F32)
        bias_v = sb(st01, "bias_v", [P, 2, B], F32)
        b2_sb = sb(st01, "b2_sb", [P, 1], F32)
        w2h = sb(st01, "w2h", [P, 2, P], F32R)
        w2l = sb(st01, "w2l", [P, 2, P], F32R)

        psum = top.enter_context(nc.psum_tensor("psum", [P, 8, 512], F32))

        s_small = sem("small_loaded")
        s_tab = sem("tables_ready")
        s_up = sem("up_loaded")
        s_bld = sem("b_loaded")
        s_apg = sem("a_rows_loaded")
        s_wraw = sem("w_sess_loaded")
        s_xc = [sem(f"x_chunk_loaded{c}") for c in range(4)]
        s_xcu = sem("x_chunk_used")
        s_draw = sem("down_loaded")
        s_gmm = sem("g_product")
        s_ghi = sem("g_high")
        s_gsp = sem("g_split")
        s_gst = sem("g_stored")
        s_bxe = sem("bx_copied")
        s_sel = sem("select_ready")
        s_bxs = sem("bx_selected")
        s_bsp = sem("bx_split")
        s_bst = sem("bx_stored")
        s_wsp = sem("w_split")
        s_wst = sem("w_stored")
        s_dhi = sem("down_high")
        s_dsp = sem("down_split")
        s_dst = sem("down_stored")
        s_dv = sem("vector_step")
        s_bmid = sem("bx_middle")
        s_tot = sem("y_totals")
        s_ph1 = sem("stage0_done")

        st0 = ExitStack()
        up_sb = sb(st0, "up_sb", [P, H, M], F32)
        arow = sb(st0, "arow", [P, NK, P], F32)
        bcol = sb(st0, "bcol", [P, NK, P], F32)
        xch = sb(st0, "xch", [P, 4, 4, GT], F32)
        gpart = sb(st0, "gpart", [P, 2, 3, HQ, M], BF16)
        grest = sb(st0, "grest", [P, M], F32)
        bx_sb = sb(st0, "bx_sb", [P, GT], F32)
        bxp = sb(st0, "bxp", [P, 3, GT], BF16)
        bxrest = sb(st0, "bxrest", [P, GT], F32)
        sel = sb(st0, "sel", [P, GB, P], F32)
        expand_sb = sb(st0, "expand_sb", [P, P], F32)
        amask = sb(st0, "amask", [P, B], F32)
        cmask = sb(st0, "cmask", [P, B], F32)
        w_idx = sb(st0, "w_idx", [P, B], I32)
        wraw = sb(st0, "wraw", [P, GB, HID], F32)
        wsp = sb(st0, "wsp", [P, GB, 2, HID], F32R)
        draw = sb(st0, "draw", [P, 2, MT * P], F32)
        dsp = sb(st0, "dsp", [P, 2, 2, MT * P], F32R)
        w2raw = sb(st0, "w2raw", [P, 2, P], F32)
        ad_i = sb(st0, "ad_i", [P, B], I32)
        se_i = sb(st0, "se_i", [P, B], I32)
        cl_i = sb(st0, "cl_i", [P, B], I32)
        tl_i = sb(st0, "tl_i", [P, B], I32)
        pr_i = sb(st0, "pr_i", [P, D], I32)
        bs_sb = sb(st0, "bs_sb", [P, 2, NS], F32)
        seq = sb(st0, "seq", [P, NS, B], F32)
        pmod = sb(st0, "pmod", [P, NK], I32)
        st0.close()

        st1 = ExitStack()
        dwt = sb(st1, "dwt", [P, HQ, 2, MT, P], F32R)
        gw = sb(st1, "gw", [P, 2, GB, HQ, M], BF16)
        bxw = sb(st1, "bxw", [P, 2, GT], BF16)
        xt = sb(st1, "xt", [P, 2, HQ, GT], F32)
        xch_ = sb(st1, "x1c_h", [P, 2, GB, HQ * P], F32R)
        xcl_ = sb(st1, "x1c_l", [P, 2, GB, HQ * P], F32R)
        ws = sb(st1, "ws", [P, 2, GB, 2, HID], F32R)
        raw = sb(st1, "act_raw", [P, 3, 2, 512], F32)
        ah = sb(st1, "act_h", [P, 2, 3, 2, 512], F32R)
        al = sb(st1, "act_l", [P, 2, 3, 2, 512], F32R)
        yb = sb(st1, "y_biased", [P, 512], F32)
        ym = sb(st1, "y_masked", [P, 512], F32)
        yt = sb(st1, "y_turned", [P, 2, HQ, P], F32)
        st_idx = sb(st1, "step_idx", [P, 2, HQ], I32)
        st1.close()
        st01.close()

        U = [psum[:, 0:2, :], psum[:, 2:4, :]]
        DN, TX, YP, TY = (psum[:, b, :] for b in range(4, 8))

        s_gld = [sem(f"g_loaded{n}") for n in range(2)]
        s_wld = [sem(f"w_loaded{n}") for n in range(2)]
        s_dld = [sem(f"down_parts_loaded{n}") for n in range(HQ)]
        s_xld = [sem(f"x_rows_loaded{n}") for n in range(2)]
        s_x1st = [sem(f"x1_rows_stored{n}") for n in range(2)]
        s_seen = sem("pool_waited")
        s_idx = sem("step_idx_ready")
        s_u = sem("hidden_product")
        s_gl = sem("gelu_done")
        s_gh = sem("gelu_high")
        s_gs = sem("gelu_split")
        s_dn = sem("down_product")
        s_x1 = sem("x1_ready")
        s_tx = sem("x1_turned")
        s_xh = sem("x1c_high")
        s_xl = sem("x1c_split")
        s_m1 = sem("mixer_product")
        s_gl1 = sem("mixer_gelu")
        s_gh1 = sem("mixer_high")
        s_gs1 = sem("mixer_split")
        s_m2 = sem("y_product")
        s_yb = sem("y_bias_added")
        s_ym = sem("y_mask_applied")
        s_ty = sem("y_turned_product")
        s_ye = sem("y_turned_copied")
        s_yst = [sem(f"y_stored{n}") for n in range(2)]

        st2 = ExitStack()
        q_sb = sb(st2, "q_sb", [P, NK, D], F32R)
        sum_sb = sb(st2, "sum_sb", [P, NG, GT], F32)
        yr = sb(st2, "yr", [P, 4, GT], F32)
        yh = sb(st2, "yh", [P, 4, GT], F32R)
        yl = sb(st2, "yl", [P, 4, GT], F32R)
        ones = sb(st2, "ones", [P, P], F32)
        sdiag = sb(st2, "sdiag", [P, 2, P], F32)
        ytot = sb(st2, "ytot", [P, B], F32)
        st2q = ExitStack()
        qraw = sb(st2q, "qraw", [P, 2, D], I32)
        st2q.close()
        dt_ = sb(st2, "dense_t", [P, 8, GT], F32)
        x1r = sb(st2, "x1r", [P, 4, GT], F32)
        st2.close()

        s_ph2 = sem("stage1_done")
        s_q = [sem(f"q_rows_loaded{n}") for n in range(2)]
        s_qb = sem("q_bits")
        s_qf = sem("q_ready")
        s_sd = sem("sum_diag")
        s_sm = sem("sum_product")
        s_se = sem("sum_copied")
        s_yld = [sem(f"y_loaded{n}") for n in range(4)]
        s_yh = sem("y_high")
        s_ysp = sem("y_split")
        s_yu = sem("y_used")
        s_x1l = [sem(f"x1_loaded{n}") for n in range(4)]
        s_acc = sem("dense_product")
        s_t = sem("zero_point_applied")
        s_du = sem("scale_applied")
        s_o = sem("out_ready")
        s_os = [sem(f"out_stored{n}") for n in range(8)]

        block = top.enter_context(nc.Block())
        SMALL = 16 * 13

        def wait_y_used(eng, g, half, k):
            hh = 2 * g + half
            if k >= 4:
                wait(eng, s_yu, hh * (NK - 1) + k - 3)
            elif not (isinstance(hh, int) and hh == 0):
                if k < 3:
                    eng.wait_ge(s_yu, (hh - 1) * (NK - 1) + k + NK - 3)
                else:
                    eng.wait_ge(s_acc, hh * 8)

        def enter_stage1(eng):
            eng.wait_ge(s_ph1, 5)

        @block.sync
        def _(sp):
            for dst, src in ((perm_sb, perm), (ad_i, adapter), (se_i, session), (cl_i, chan_len),
                             (tl_i, time_len), (rows_sb, rows), (ident_sb, ident),
                             (expand_sb, expand), (pr_i, perm_row), (b2_sb, b2)):
                sp.dma_start(dst[:], src[:]).then_inc(s_small, 16)
            sp.dma_start(bs_sb[:].rearrange("p a b -> p (a b)"), b_sess[:]).then_inc(s_small, 16)
            sp.dma_start(dense_sb[:].rearrange("p a b -> p (a b)"), dense[:]).then_inc(s_small, 16)
            sp.dma_start(w2raw[:].rearrange("p a b -> p (a b)"), w2[:]).then_inc(s_small, 16)
            for h in range(0, H, HQ):
                sp.dma_start(up_sb[:, h:h + HQ, :].rearrange("p h m -> p (h m)"),
                             up[:, h * M:(h + HQ) * M]).then_inc(s_up, 16)
            sp.dma_start(bcol[:], bdown.rearrange("(k p) r -> p k r", p=P)).then_inc(s_bld, 16)

            def load_chunk(g, c):
                src = xT[bass.ds(g * D + c * 4 * P, 4 * P), :].rearrange("(k p) t -> p k t", p=P)
                sp.dma_start(xch[:, c, :, :], src).then_inc(s_xc[c], 16)

            def load_down(g):
                sp.dma_start(draw[:].rearrange("p a m -> p (a m)"),
                             down[:, bass.ds(g * 2 * MT * P, 2 * MT * P)]).then_inc(s_draw, 16)

            for c in range(4):
                load_chunk(0, c)
            load_down(0)
            with sp.Fori(1, NG) as g:
                for c in range(4):
                    sp.wait_ge(s_xcu, 4 * g - 3 + c)
                    load_chunk(g, c)
                sp.wait_ge(s_dsp, g)
                load_down(g)
            sp.wait_ge(s_draw, 16 * NG)
            for c in range(4):
                sp.wait_ge(s_xc[c], 16 * NG)
            sp.sem_inc(s_ph1, 1)
            enter_stage1(sp)

            g_entries = g_idx[0:1, :, :].rearrange("p q b -> p (q b)")

            def load_g(it, g, par, free):
                entry = [sp.value_load(g_entries[:, bass.ds(it * GB + b, 1)], min_val=0, max_val=NQ * NA - 1)
                         for b in range(GB)]
                g = g if isinstance(g, int) else sp.snap(g)
                wait(sp, s_u, free)
                sp.dma_start(bxw[:, par, :],
                             bx_dram[bass.ds(g, 1), :, :].rearrange("o p m -> (o p) m")).then_inc(s_gld[par], 16)
                for b in range(GB):
                    sp.dma_start(gw[0:KG, par, b, :, :].rearrange("p h m -> p (h m)"),
                                 g_dram[bass.ds(entry[b], 1), :, :].rearrange("o p m -> (o p) m")).then_inc(s_gld[par], 16)

            def load_w(g, par, free):
                g = g if isinstance(g, int) else sp.snap(g)
                wait(sp, s_m1, free)
                sp.dma_start(ws[:, par, :, :, :].rearrange("p b x h -> p b (x h)").bitcast(F32),
                             ws_dram[bass.ds(g * GB, GB), :, :].rearrange("b p h -> p b h")).then_inc(s_wld[par], 16)

            load_g(0, 0, 0, 0)
            for q in range(NQ):
                for hq in range(HQ):
                    wait(sp, s_dn, (STEPS // NQ * q - HQ + 1 + hq) if q else 0)
                    sp.dma_start(dwt[:, hq, :, :, :].rearrange("p x m d -> p (x m d)").bitcast(F32),
                                 dw_dram[q * HQ + hq, :, :]).then_inc(s_dld[hq], 16)

                def iteration(j, par):
                    it = NG * q + 2 * j + par
                    if not (isinstance(j, int) and it == NIT - 1):
                        load_g(it + 1, (2 * j + par + 1) % NG, 1 - par, 2 * HQ * it)
                    load_w(2 * j + par, par, HQ * (it - 1))

                iteration(0, 0)
                iteration(0, 1)
                with sp.Fori(1, NG // 2 - 1) as j:
                    iteration(j, 0)
                    iteration(j, 1)
                iteration(NG // 2 - 1, 0)
                iteration(NG // 2 - 1, 1)

            sp.wait_ge(s_ph2, 4)

            def load_half(g, half):
                for k in range(NK):
                    n = k % 4
                    it = g + NG * (k // HQ)
                    it = it if isinstance(it, int) else sp.snap(it)
                    wait(sp, s_ysp, (2 * g + half) * NK + k - 3)
                    sp.dma_start(yr[:, n, :],
                                 y_dram[bass.ds(it, 1), :, k % HQ, :].rearrange("o p t -> (o p) t")).then_inc(s_yld[n], 16)
                    if 6 <= k < 14 and not (isinstance(g, int) and g == 0 and half == 0):
                        load_x1(g, half, k - 6)

            def load_x1(g, half, n):
                row = g * D + (half - 1) * 8 * P + n * P
                row = row if isinstance(row, int) else sp.snap(row)
                if n == 0 and isinstance(g, int):
                    sp.wait_ge(s_qf, NK)
                wait(sp, s_o, (2 * g + half - 1) * 8 + n - 3)
                sp.dma_start(x1r[:, n % 4, :], x1_dram[bass.ds(row, P), :]).then_inc(s_x1l[n % 4], 16)

            load_half(0, 0)
            load_half(0, 1)
            with sp.Fori(1, NG) as g:
                load_half(g, 0)
                load_half(g, 1)
            for n in range(8):
                load_x1(NG, 0, n)
            for n in range(8):
                sp.wait_ge(s_os[n], 16 * NG * 2)

        @block.gpsimd
        def _(pool):
            pool.wait_ge(s_small, SMALL)
            for k in range(NK):
                nc.gpsimd.indirect_dma_start(
                    arow[:, k, :], None, adown[:],
                    bass.IndirectOffsetOnAxis(ap=perm_sb[:, k:k + 1], axis=0)).then_inc(s_apg, 16)
            pool.wait_ge(s_tab, 1)
            for b in range(B):
                if b % GB == 0:
                    wait(pool, s_wsp, b // GB)
                nc.gpsimd.indirect_dma_start(
                    wraw[:, b % GB, :], None, w_sess[:],
                    bass.IndirectOffsetOnAxis(ap=w_idx[:, b:b + 1], axis=0)).then_inc(s_wraw, 16)
            pool.wait_ge(s_apg, 16 * NK)
            pool.wait_ge(s_wraw, 16 * B)
            pool.sem_inc(s_ph1, 1)
            enter_stage1(pool)

            def gather_x(it, par, n):
                nc.gpsimd.tensor_copy(st_idx[:, par, :], row_idx[:, bass.ds(it, 1), :].rearrange("p o h -> p (o h)")).then_inc(s_idx, 1)
                pool.wait_ge(s_idx, n)
                pool.sem_inc(s_seen, 1)
                for hq in range(HQ):
                    nc.gpsimd.indirect_dma_start(
                        xt[:, par, hq, :], None, xT[:],
                        bass.IndirectOffsetOnAxis(ap=st_idx[:, par, hq:hq + 1], axis=0)).then_inc(s_xld[par], 16)

            def scatter_x1(it, par):
                for hq in range(HQ):
                    pool.wait_ge(s_x1, HQ * it + hq + 1)
                    pool.sem_inc(s_seen, 1)
                    nc.gpsimd.indirect_dma_start(
                        x1_dram[:], bass.IndirectOffsetOnAxis(ap=st_idx[:, par, hq:hq + 1], axis=0),
                        xt[:, par, hq, :], None).then_inc(s_x1st[par], 16)

            gather_x(0, 0, 1)
            gather_x(1, 1, 2)
            with pool.Fori(0, NIT // 2 - 1) as j:
                for par in range(2):
                    scatter_x1(2 * j + par, par)
                    pool.wait_ge(s_tx, HQ * (2 * j + par + 1))
                    pool.wait_ge(s_x1st[par], 16 * HQ * (j + 1))
                    pool.sem_inc(s_seen, 1)
                    gather_x(2 * j + par + 2, par, 2 * j + par + 3)
            scatter_x1(NIT - 2, 0)
            scatter_x1(NIT - 1, 1)
            for par in range(2):
                pool.wait_ge(s_x1st[par], 16 * HQ * NIT // 2)
            pool.sem_inc(s_ph2, 1)
            pool.wait_ge(s_ph2, 4)
            for k in range(NK):
                wait(pool, s_qf, k - 1)
                nc.gpsimd.indirect_dma_start(
                    qraw[:, k % 2, :], None, qw[:],
                    bass.IndirectOffsetOnAxis(ap=perm_sb[:, k:k + 1], axis=0)).then_inc(s_q[k % 2], 16)
            with pool.Fori(0, 2 * NG) as hh:
                for n in range(8):
                    row = pool.snap(hh * 8 * P + n * P)
                    pool.wait_ge(s_o, hh * 8 + n + 1)
                    pool.sem_inc(s_seen, 1)
                    pool.dma_start(out[bass.ds(row, P), :], dt_[:, n, :]).then_inc(s_os[n], 16)

        @block.tensor
        def _(pe):
            for h in range(H):
                if h % HQ == 0:
                    pe.wait_ge(s_up, 16 * NQ)
                if h == 0:
                    pe.wait_ge(s_apg, 16 * NK)
                wait(pe, s_gsp, h - 1)
                nc.tensor.matmul(psum[:, h % 2, :], arow[:, h, :], up_sb[:, h, :],
                                 start=True, stop=True).then_inc(s_gmm, 1)
            pe.wait_ge(s_bld, 16)
            def adapter_rows(g):
                wait(pe, s_bxe, g)
                for k in range(NK):
                    if k % 4 == 0:
                        pe.wait_ge(s_xc[k // 4], 16 * g + 16)
                    mm = nc.tensor.matmul(psum[:, 2, :], bcol[:, k, :], xch[:, k // 4, k % 4, :],
                                          start=(k == 0), stop=(k == NK - 1))
                    if k % 4 == 3:
                        mm.then_inc(s_xcu, 1)
                pe.wait_ge(s_bxe, g + 1)
                pe.wait_ge(s_sel, g + 1)
                wait(pe, s_bsp, g)
                for b in range(GB):
                    mm = nc.tensor.matmul(psum[:, 3, b * C:(b + 1) * C], sel[:, b, :],
                                          bx_sb[:, b * C:(b + 1) * C], start=True, stop=True)
                mm.then_inc(s_bxs, 1)

            adapter_rows(0)
            with pe.Fori(1, NG) as g:
                adapter_rows(g)
            pe.wait_ge(s_bsp, NG)
            pe.sem_inc(s_ph1, 1)
            enter_stage1(pe)

            def hidden(i, k, part):
                it_par, hq = k // HQ, k % HQ
                u = U[(k + part) % 2]
                for m in range(2):
                    for b in range(GB):
                        col = (2 * part + m) * P
                        mm = nc.tensor.matmul(u[:, m, b * C:(b + 1) * C], gw[0:KG, it_par, b, hq, col:col + P],
                                              bxw[0:KG, it_par, b * C:(b + 1) * C],
                                              start=True, stop=True)
                mm.then_inc(s_u, 1)

            def step(i, k):
                s = UNROLL * i + k
                now, dn, tx = earlier(i, k, 0), earlier(i, k, 1), earlier(i, k, 2)
                m1, m2, ty = earlier(i, k, 6), earlier(i, k, 7), earlier(i, k, 8)
                if now:
                    if k % HQ == 0:
                        pe.wait_ge(s_gld[k // HQ], 16 * (GB + 1) * (i + 1))
                    wait(pe, s_gl, 2 * s)
                    hidden(i, k, 0)
                if ty:
                    v = UNROLL * ty[0] + ty[1]
                    pe.wait_ge(s_ym, v + 1)
                    wait(pe, s_ye, v + CREDIT)
                    for t in range(HQ):
                        mm = nc.tensor.transpose(TY[:, t * P:(t + 1) * P], ym[:, t * P:(t + 1) * P], ident_sb[:])
                    mm.then_inc(s_ty, 1)
                if tx:
                    j = UNROLL * tx[0] + tx[1]
                    pe.wait_ge(s_x1, j + 1)
                    wait(pe, s_xl, j)
                    for b in range(GB):
                        mm = nc.tensor.transpose(TX[:, b * C:(b + 1) * C],
                                                 xt[:, tx[1] // HQ, tx[1] % HQ, b * C:(b + 1) * C], ident_sb[:])
                    mm.then_inc(s_tx, 1)
                if now:
                    if earlier(i, k, 7):
                        pe.wait_ge(s_gl1, s - 6)
                    hidden(i, k, 1)
                if dn:
                    j = UNROLL * dn[0] + dn[1]
                    par, hq = dn[1] // HQ, dn[1] % HQ
                    if par == 0:
                        pe.wait_ge(s_dld[hq], 16 * (dn[0] // (NG // 2) + 1))
                    pe.wait_ge(s_gs, 2 * j + 2)
                    wait(pe, s_x1, j)
                    n = 0
                    for m in range(MT):
                        for w, a in ((0, ah), (1, ah), (0, al)):
                            mm = nc.tensor.matmul(DN, dwt[:, hq, w, m, :], a[:, dn[1] % 2, m // 2, m % 2, :],
                                                  start=(n == 0), stop=(n == 3 * MT - 1))
                            n += 1
                    mm.then_inc(s_dn, 1)
                if m2:
                    v = UNROLL * m2[0] + m2[1]
                    pe.wait_ge(s_gs1, v + 1)
                    wait(pe, s_yb, v)
                    n = 0
                    for x in range(2):
                        for w, a in ((w2h, ah), (w2l, ah), (w2h, al)):
                            mm = nc.tensor.matmul(YP, w[:, x, :], a[:, m2[1] % 2, 2, x, :],
                                                  start=(n == 0), stop=(n == 5))
                            n += 1
                    mm.then_inc(s_m2, 1)
                if m1:
                    v = UNROLL * m1[0] + m1[1]
                    par, b = m1[1] // GB, m1[1] % GB
                    if b == 0:
                        pe.wait_ge(s_wld[par], 16 * (m1[0] + 1))
                        pe.wait_ge(s_xl, v + GB)
                    if now:
                        pe.wait_ge(s_gl, 2 * s + 1)
                    else:
                        pe.wait_ge(s_gl, 2 * STEPS)
                        pe.wait_ge(s_gl1, v - 1)
                    u = U[k % 2]
                    for x in range(2):
                        n = 0
                        for w, a in ((0, xch_), (1, xch_), (0, xcl_)):
                            mm = nc.tensor.matmul(u[:, x, :], ws[:, par, b, w, x * P:(x + 1) * P],
                                                  a[:, par, b, :], start=(n == 0), stop=(n == 2))
                            n += 1
                    mm.then_inc(s_m1, 1)

            pe.sem_inc(s_m2, CREDIT)
            step_loop(pe, step, 8)
            pe.sem_inc(s_ph2, 1)
            pe.wait_ge(s_ph2, 4)

            for b in range(B):
                pe.wait_ge(s_sd, b + 2)
                bank = b // GB
                mm = nc.tensor.matmul(psum[:, bank, b % GB * C:(b % GB + 1) * C], ones[:], sdiag[:, b % 2, :],
                                      start=True, stop=True)
                mm.then_inc(s_sm, 1)

            def dense_group(g):
                for half in range(2):
                    for k in range(NK):
                        pe.wait_ge(s_qf, k + 1)
                        pe.wait_ge(s_ysp, g * 2 * NK + half * NK + k + 1)
                        for n in range(8):
                            if k == 0:
                                if half == 0 and isinstance(g, int):
                                    pe.wait_ge(s_se, n + 1)
                                else:
                                    pe.wait_ge(s_t, g * NK + half * 8 + n - 7)
                            col = (half * 8 + n) * P
                            nc.tensor.matmul(psum[:, n, :], q_sb[:, k, col:col + P], yh[:, k % 4, :],
                                             start=(k == 0), stop=False)
                            mm = nc.tensor.matmul(psum[:, n, :], q_sb[:, k, col:col + P], yl[:, k % 4, :],
                                                  start=False, stop=(k == NK - 1))
                            if k == NK - 1:
                                mm.then_inc(s_acc, 1)
                            elif n == 7:
                                mm.then_inc(s_yu, 1)
            dense_group(0)
            with pe.Fori(1, NG) as g:
                dense_group(g)

        @block.scalar
        def _(act):
            for h in range(H):
                q, hq = h // HQ, h % HQ
                act.wait_ge(s_gmm, h + 1)
                if hq == 0:
                    wait(act, s_gst, 16 * 7 * q)
                nc.scalar.activation(gpart[:, q % 2, 0, hq, :], psum[:, h % 2, :], ACT.Copy).then_inc(s_ghi, 1)
                if hq == HQ - 1:
                    act.wait_ge(s_gsp, h + 1)
                    for grp, part in enumerate((0, 1, 0, 1, 0, 1, 2)):
                        act.dma_start(g_dram[q * NA:(q + 1) * NA, grp * R:(grp + 1) * R, :],
                                      gpart[:, q % 2, part, :, :].rearrange("p h m -> p (h m)")).then_inc(s_gst, 16)
            def prepare(g):
                act.wait_ge(s_draw, 16 * g + 16)
                wait(act, s_dst, 16 * g)
                nc.scalar.activation(dsp[:, :, 0, :], draw[:], ACT.Copy).then_inc(s_dhi, 1)
                wait(act, s_bxs, g)
                act.wait_ge(s_xcu, 4 * g + 4)
                nc.scalar.activation(bx_sb[:], psum[:, 2, :], ACT.Copy).then_inc(s_bxe, 1)
                act.wait_ge(s_dsp, g + 1)
                act.dma_start(dw_dram[bass.ds(2 * g, 2), :, :].rearrange("h p x -> p h x"),
                              dsp[:].rearrange("p h x m -> p h (x m)").bitcast(F32)).then_inc(s_dst, 16)
                act.wait_ge(s_wsp, g + 1)
                act.dma_start(ws_dram[bass.ds(g * GB, GB), :, :].rearrange("b p h -> p b h"),
                              wsp[:].rearrange("p b x h -> p b (x h)").bitcast(F32)).then_inc(s_wst, 16)
                act.wait_ge(s_bsp, g + 1)
                for lo, part in ((0, 0), (32, 1), (64, 2), (96, 0)):
                    act.dma_start(bx_dram[bass.ds(g, 1), lo:lo + 32, :].rearrange("o p t -> (o p) t"),
                                  bxp[lo:lo + 32, part, :]).then_inc(s_bst, 16)

            prepare(0)
            with act.Fori(1, NG) as g:
                prepare(g)
            act.wait_ge(s_gst, 16 * 7 * NQ)
            act.wait_ge(s_bst, 16 * 4 * NG)
            act.wait_ge(s_wst, 16 * NG)
            act.wait_ge(s_dst, 16 * NG)
            act.sem_inc(s_ph1, 1)
            enter_stage1(act)

            def step(i, k):
                s = UNROLL * i + k
                now, tx = earlier(i, k, 0), earlier(i, k, 2)
                m1, m2, ty = earlier(i, k, 6), earlier(i, k, 7), earlier(i, k, 8)
                if now:
                    act.wait_ge(s_u, 2 * s + 1)
                    wait(act, s_gs, 2 * s - 1)
                    nc.scalar.activation(raw[:, 0, :, :], U[k % 2], ACT.Gelu).then_inc(s_gl, 1)
                if ty:
                    v = UNROLL * ty[0] + ty[1]
                    act.wait_ge(s_ty, v + 1)
                    wait(act, s_yst[k % 2], 8 * (v - ty[1] % 2) + CREDIT)
                    nc.scalar.activation(yt[:, k % 2, :, :].rearrange("p a b -> p (a b)"), TY, ACT.Copy).then_inc(s_ye, 1)
                if tx:
                    j = UNROLL * tx[0] + tx[1]
                    act.wait_ge(s_tx, j + 1)
                    if tx[1] % HQ == 0:
                        wait(act, s_m1, j - HQ)
                    dst = xch_[:, tx[1] // HQ, :, tx[1] % HQ * P:(tx[1] % HQ + 1) * P]
                    nc.scalar.activation(dst, TX.rearrange("p (b t) -> p b t", b=GB), ACT.Copy).then_inc(s_xh, 1)
                if ty:
                    act.wait_ge(s_ye, v + 1 + CREDIT)
                    y_dst = y_dram[bass.ds(2 * ty[0] + ty[1] // GB, 1), :, :, ty[1] % GB * C:(ty[1] % GB + 1) * C]
                    act.dma_start(y_dst.rearrange("o p k t -> (o p) k t"), yt[:, k % 2, :, :]).then_inc(s_yst[k % 2], 16)
                if now:
                    act.wait_ge(s_u, 2 * s + 2)
                    wait(act, s_gs, 2 * s)
                    nc.scalar.activation(raw[:, 1, :, :], U[(k + 1) % 2], ACT.Gelu).then_inc(s_gl, 1)
                if m2:
                    v = UNROLL * m2[0] + m2[1]
                    act.wait_ge(s_m2, v + 1 + CREDIT)
                    wait(act, s_ym, v)
                    nc.scalar.activation(yb[:], YP, ACT.Identity, bias=b2_sb[:, 0:1]).then_inc(s_yb, 1)
                if m1:
                    v = UNROLL * m1[0] + m1[1]
                    act.wait_ge(s_m1, v + 1)
                    wait(act, s_gs1, v)
                    b = UNROLL * (m1[0] % (NG // 2)) + m1[1]
                    for x in range(2):
                        a = nc.scalar.activation(raw[:, 2, x, :], U[k % 2][:, x, :], ACT.Gelu,
                                                 bias=bias_v[:, x, bass.ds(b, 1)])
                    a.then_inc(s_gl1, 1)

            act.sem_inc(s_ye, CREDIT)
            for n in range(2):
                act.sem_inc(s_yst[n], CREDIT)
            step_loop(act, step, 8)
            for n in range(2):
                act.wait_ge(s_yst[n], 8 * STEPS + CREDIT)
            act.sem_inc(s_ph2, 1)
            act.wait_ge(s_ph2, 4)

            for bank in range(NG):
                act.wait_ge(s_sm, GB * (bank + 1))
                nc.scalar.activation(sum_sb[:, bank, :], psum[:, bank, :], ACT.Copy).then_inc(s_se, 1)

            def unpack(k):
                act.wait_ge(s_qb, k + 1)
                nc.scalar.activation(q_sb[:, k, :], qraw[:, k % 2, :], ACT.Copy).then_inc(s_qf, 1)

            def y_high(g, half, k):
                act.wait_ge(s_yld[k % 4], 16 * (8 * g + 4 * half + k // 4 + 1))
                wait_y_used(act, g, half, k)
                nc.scalar.activation(yh[:, k % 4, :], yr[:, k % 4, :], ACT.Copy).then_inc(s_yh, 1)

            def scale(g, half):
                for n in range(8):
                    nn = 8 * (1 - half) + n
                    act.wait_ge(s_t, (2 * g + half - 1) * 8 + n + 1)
                    nc.scalar.activation(dt_[:, n, :], dt_[:, n, :], ACT.Identity, bias=dense_sb[:, 2, nn:nn + 1],
                                         scale=dense_sb[:, 0, nn:nn + 1]).then_inc(s_du, 1)

            def half_group(g, half):
                for k in range(3):
                    y_high(g, half, k)
                scale(g, half)
                for k in range(3, NK):
                    y_high(g, half, k)

            unpack(0)
            for k in range(NK):
                if k + 1 < NK:
                    unpack(k + 1)
                y_high(0, 0, k)
            half_group(0, 1)
            with act.Fori(1, NG) as g:
                half_group(g, 0)
                half_group(g, 1)
            scale(NG, 0)

        @block.vector
        def _(dve):
            done = 0

            def own(instruction):
                nonlocal done
                done += 1
                instruction.then_inc(s_dv, 1)

            def after_own():
                dve.wait_ge(s_dv, done)

            dve.wait_ge(s_small, SMALL)
            v = nc.vector
            for g in range(NG):
                own(v.tensor_scalar(row_idx[:, :, :].rearrange("p (q g) h -> p q g h", g=NG)[:, :, g, :],
                                    perm_sb[:].rearrange("p (q h) -> p q h", h=HQ), g * D, None, ALU.add))
            for q in range(NQ):
                own(v.tensor_scalar(g_idx[:, q, :], ad_i[:], q * NA, None, ALU.add))
            own(v.tensor_scalar(w_idx[:], se_i[:], C, rows_sb[:, 0:1], ALU.mult, ALU.add))
            own(v.tensor_scalar(amask[:], ad_i[:], rows_sb[:, 1:2], None, ALU.is_equal))
            own(v.tensor_scalar(cmask[:], cl_i[:], rows_sb[:, 0:1], None, ALU.is_gt))
            own(v.tensor_copy(time_f[:], tl_i[:]))
            own(v.tensor_copy(permrow_f[:], pr_i[:]))
            own(v.tensor_scalar(nzero[:], dense_sb[:, 1, :], -1.0, None, ALU.mult))
            own(v.tensor_scalar(pmod[:], perm_sb[:], 3, None, ALU.bitwise_and))
            own(v.memset(bias_v[:], 0.0))
            for n in range(NS):
                own(v.tensor_scalar(seq[:, n, :], se_i[:], n, None, ALU.is_equal))
            own(v.tensor_copy(w2h[:], w2raw[:]))
            after_own()
            own(v.tensor_scalar(shift[:], pmod[:], 1, 6, ALU.is_equal, ALU.mult))
            own(v.tensor_tensor(w2l[:], w2raw[:], w2h[:].bitcast(F32), ALU.subtract))
            for n in range(NS):
                for x in range(2):
                    own(v.scalar_tensor_tensor(bias_v[:, x, :], seq[:, n, :], bs_sb[:, x, n:n + 1],
                                               bias_v[:, x, :], ALU.mult, ALU.add))
                after_own()
            v.tensor_copy(seq[:, 0, :], seq[:, 1, :]).then_inc(s_tab, 1)

            for h in range(H):
                q, hq = h // HQ, h % HQ
                part = gpart[:, q % 2, :, hq, :]
                dve.wait_ge(s_ghi, h + 1)
                own(v.tensor_tensor(grest[:], psum[:, h % 2, :], part[:, 0, :], ALU.subtract))
                after_own()
                own(v.tensor_copy(part[:, 1, :], grest[:]))
                after_own()
                v.tensor_tensor(part[:, 2, :], grest[:], part[:, 1, :], ALU.subtract).then_inc(s_gsp, 1)
                dve.wait_ge(s_gsp, h + 1)

            dve.wait_ge(s_tab, 1)
            base = done

            def prepare(g):
                wait(dve, s_bxs, g)
                for b in range(GB):
                    a = v.tensor_scalar(sel[:, b, :], expand_sb[:], amask[:, bass.ds(g * GB + b, 1)], None, ALU.mult)
                a.then_inc(s_sel, 1)
                dve.wait_ge(s_dhi, g + 1)
                v.tensor_tensor(dsp[:, :, 1, :], draw[:], dsp[:, :, 0, :].bitcast(F32), ALU.subtract).then_inc(s_dsp, 1)
                dve.wait_ge(s_wraw, 16 * GB * g + 16 * GB)
                wait(dve, s_wst, 16 * g)
                for b in range(GB):
                    a = v.tensor_scalar(wsp[:, b, 0, :], wraw[:, b, :], cmask[:, bass.ds(g * GB + b, 1)], None, ALU.mult)
                a.then_inc(s_dv, 1)
                dve.wait_ge(s_dv, 3 * g + (base + 1))
                for b in range(GB):
                    a = v.scalar_tensor_tensor(wsp[:, b, 1, :], wraw[:, b, :], cmask[:, bass.ds(g * GB + b, 1)],
                                               wsp[:, b, 0, :].bitcast(F32), ALU.mult, ALU.subtract)
                a.then_inc(s_wsp, 1)
                dve.wait_ge(s_bxs, g + 1)
                wait(dve, s_bst, 64 * g)
                v.tensor_copy(bxp[:, 0, :], psum[:, 3, :]).then_inc(s_dv, 1)
                dve.wait_ge(s_dv, 3 * g + (base + 2))
                v.tensor_tensor(bxrest[:], psum[:, 3, :], bxp[:, 0, :], ALU.subtract).then_inc(s_dv, 1)
                dve.wait_ge(s_dv, 3 * g + (base + 3))
                v.tensor_copy(bxp[:, 1, :], bxrest[:]).then_inc(s_bmid, 1)
                dve.wait_ge(s_bmid, g + 1)
                v.tensor_tensor(bxp[:, 2, :], bxrest[:], bxp[:, 1, :], ALU.subtract).then_inc(s_bsp, 1)
                dve.wait_ge(s_bsp, g + 1)

            prepare(0)
            with dve.Fori(1, NG) as g:
                prepare(g)
            dve.wait_ge(s_wsp, NG)
            dve.wait_ge(s_dsp, NG)
            dve.sem_inc(s_ph1, 1)
            enter_stage1(dve)

            def split(par, slot, half, high_sem, high_count, split_sem):
                v.tensor_copy(ah[:, par, slot, :, :], raw[:, half, :, :]).then_inc(high_sem, 1)
                dve.wait_ge(high_sem, high_count)
                v.tensor_tensor(al[:, par, slot, :, :], raw[:, half, :, :],
                                ah[:, par, slot, :, :].bitcast(F32), ALU.subtract).then_inc(split_sem, 1)

            def step(i, k):
                s = UNROLL * i + k
                now, dn, tx = earlier(i, k, 0), earlier(i, k, 1), earlier(i, k, 2)
                m2 = earlier(i, k, 7)
                if m2:
                    v2 = UNROLL * m2[0] + m2[1]
                    dve.wait_ge(s_gl1, v2 + 1)
                    wait(dve, s_m2, v2 - 1 + CREDIT)
                    split(m2[1] % 2, 2, 2, s_gh1, v2 + 1, s_gs1)
                if now:
                    dve.wait_ge(s_gl, 2 * s + 1)
                    wait(dve, s_dn, s - 1)
                    split(k % 2, 0, 0, s_gh, 2 * s + 1, s_gs)
                if tx:
                    j = UNROLL * tx[0] + tx[1]
                    dve.wait_ge(s_xh, j + 1)
                    cols = slice(tx[1] % HQ * P, (tx[1] % HQ + 1) * P)
                    par = tx[1] // HQ
                    v.tensor_tensor(xcl_[:, par, :, cols], TX.rearrange("p (b t) -> p b t", b=GB),
                                    xch_[:, par, :, cols].bitcast(F32), ALU.subtract).then_inc(s_xl, 1)
                if now:
                    dve.wait_ge(s_gl, 2 * s + 2)
                    split(k % 2, 1, 1, s_gh, 2 * s + 2, s_gs)
                if dn:
                    j = UNROLL * dn[0] + dn[1]
                    par, hq = dn[1] // HQ, dn[1] % HQ
                    dve.wait_ge(s_dn, j + 1)
                    dve.wait_ge(s_xld[par], 16 * HQ * (dn[0] + 1))
                    v.tensor_tensor(xt[:, par, hq, :], xt[:, par, hq, :], DN, ALU.add).then_inc(s_x1, 1)
                if m2:
                    dve.wait_ge(s_yb, v2 + 1)
                    wait(dve, s_ty, v2)
                    b = UNROLL * (m2[0] % (NG // 2)) + m2[1]
                    v.scalar_tensor_tensor(ym[:], permrow_f[:, bass.ds(m2[0] // (NG // 2) * HQ * P, HQ * P)],
                                           time_f[:, bass.ds(b, 1)], yb[:], ALU.is_lt, ALU.mult,
                                           accum_out=ysum[:, bass.ds(v2, 1)]).then_inc(s_ym, 1)

            step_loop(dve, step, 8)
            for watched, count in ((s_x1, STEPS), (s_ym, STEPS), (s_xl, STEPS), (s_gs1, STEPS)):
                dve.wait_ge(watched, count)
            dve.sem_inc(s_ph2, 1)
            dve.wait_ge(s_ph2, 4)

            v.memset(ones[:], 1.0).then_inc(s_sd, 1)
            n_tot = 0
            ys = ysum[:].rearrange("p (q b) -> p q b", b=B)
            for a, b in ((ys[:, 0, :], ys[:, 1, :]), (ytot[:], ys[:, 2, :]), (ytot[:], ys[:, 3, :])):
                v.tensor_tensor(ytot[:], a, b, ALU.add).then_inc(s_tot, 1)
                n_tot += 1
                dve.wait_ge(s_tot, n_tot)
            for b in range(B):
                wait(dve, s_sm, b - 1)
                v.tensor_scalar(sdiag[:, b % 2, :], ident_sb[:], ytot[:, b:b + 1], None, ALU.mult).then_inc(s_sd, 1)

            def bits(k):
                dve.wait_ge(s_q[k % 2], 16 * (k // 2 + 1))
                v.tensor_scalar(qraw[:, k % 2, :], qraw[:, k % 2, :], shift[:, k:k + 1], 63,
                                ALU.logical_shift_right, ALU.bitwise_and).then_inc(s_qb, 1)

            def y_low(g, half, k):
                dve.wait_ge(s_yh, (2 * g + half) * NK + k + 1)
                v.tensor_tensor(yl[:, k % 4, :], yr[:, k % 4, :], yh[:, k % 4, :].bitcast(F32),
                                ALU.subtract).then_inc(s_ysp, 1)

            def zero_point(g, half):
                last_g = g - 1 if half == 0 else g
                for n in range(8):
                    nn = 8 * (1 - half) + n
                    dve.wait_ge(s_acc, (2 * g + half - 1) * 8 + n + 1)
                    wait(dve, s_os[n], 16 * (2 * g + half - 1))
                    v.scalar_tensor_tensor(dt_[:, n, :], sum_sb[:, bass.ds(last_g, 1), :].rearrange("p o t -> p (o t)"),
                                           nzero[:, nn:nn + 1], psum[:, n, :], ALU.mult, ALU.add).then_inc(s_t, 1)

            def add_x1(g, half, n):
                e = (2 * g + half - 1) * 8 + n
                dve.wait_ge(s_du, e + 1)
                dve.wait_ge(s_x1l[n % 4], 16 * (2 * (2 * g + half - 1) + n // 4 + 1))
                v.tensor_tensor(dt_[:, n, :], dt_[:, n, :], x1r[:, n % 4, :], ALU.add).then_inc(s_o, 1)

            def half_group(g, half):
                for k in range(3):
                    y_low(g, half, k)
                zero_point(g, half)
                for k in range(3, NK):
                    y_low(g, half, k)
                    if 5 <= k < 13:
                        add_x1(g, half, k - 5)

            bits(0)
            for k in range(NK):
                if k + 1 < NK:
                    bits(k + 1)
                y_low(0, 0, k)
            half_group(0, 1)
            with dve.Fori(1, NG) as g:
                half_group(g, 0)
                half_group(g, 1)
            zero_point(NG, 0)
            for n in range(8):
                add_x1(NG, 0, n)


def kernel(x, itok_B_3_7, itok_B_0_7, itok_B_2182_4065, _lenS, L0_cond_A, L0_cond_B, L0_ffn_up, L0_ffn_down,
           L0_ffn_perm, L1_cond_W_sess, L1_cond_b_sess, L1_cond_W2, L1_cond_b2, L1_ffn_qweight,
           L1_ffn_weight_scale, L1_ffn_weight_zero_point, L1_ffn_bias):
    import concourse.bacc as bacc
    from concourse.bass_utils import run_bass_kernel_spmd

    def spread(a):
        a = np.asarray(a)
        return np.ascontiguousarray(np.broadcast_to(a[None, :], (P, a.shape[0])))

    def columns(a):
        return np.asarray(a).reshape(NK, P).T

    k = np.arange(D)
    word = 3 * (k // 4) + np.array([0, 0, 1, 2])[k % 4]
    p = np.arange(P)
    arrays = {
        "xT": np.asarray(x).reshape(NG, GT, D).transpose(0, 2, 1).reshape(NG * D, GT),
        "adown": np.asarray(L0_cond_A).transpose(1, 0, 2).reshape(D, NA * R),
        "bdown": np.asarray(L0_cond_B).transpose(2, 0, 1).reshape(D, NA * R),
        "up": np.asarray(L0_ffn_up).transpose(1, 0, 2).reshape(P, H * M),
        "down": np.asarray(L0_ffn_down).reshape(H, MT, P, P).transpose(2, 0, 1, 3).reshape(P, H * MT * P),
        "w_sess": np.asarray(L1_cond_W_sess).reshape(NS * C, HID),
        "b_sess": np.asarray(L1_cond_b_sess).reshape(NS, 2, P).transpose(2, 1, 0).reshape(P, 2 * NS),
        "w2": np.asarray(L1_cond_W2).reshape(2, P, P).transpose(1, 0, 2).reshape(P, 2 * P),
        "b2": np.asarray(L1_cond_b2).reshape(P, 1),
        "qw": np.asarray(L1_ffn_qweight).T[word],
        "dense": np.stack([columns(L1_ffn_weight_scale), columns(L1_ffn_weight_zero_point),
                           columns(L1_ffn_bias)], axis=1).reshape(P, 3 * NK),
        "perm": columns(L0_ffn_perm),
        "perm_row": spread(L0_ffn_perm),
        "adapter": spread(itok_B_3_7),
        "session": spread(itok_B_0_7),
        "chan_len": spread(_lenS),
        "time_len": spread(itok_B_2182_4065),
        "ident": np.eye(P, dtype=np.float32),
        "expand": (p[:, None] % R == p[None, :] % R).astype(np.float32),
        "rows": np.stack([p, p // R], axis=1).astype(np.float32),
    }
    arrays = {name: np.ascontiguousarray(a) for name, a in arrays.items()}
    nc = bacc.Bacc("TRN2", target_bir_lowering=False, num_devices=1)
    args = {name: nc.dram_tensor(name, a.shape, mybir.dt.from_np(a.dtype), kind="ExternalInput").ap()
            for name, a in arrays.items()}
    out = nc.dram_tensor("out", [NG * D, GT], F32, kind="ExternalOutput").ap()
    build(nc, **args, out=out)
    result = run_bass_kernel_spmd(nc, [arrays], core_ids=[0]).results[0]["out"]
    return result.reshape(NG, D, GT).transpose(0, 2, 1).reshape(B, C, D)
```

```python
from contextlib import ExitStack

import numpy as np

import concourse.bass as bass
from concourse import mybir

F32 = mybir.dt.float32
F32R = mybir.dt.float32r
BF16 = mybir.dt.bfloat16
I32 = mybir.dt.int32
ALU = mybir.AluOpType
ACT = mybir.ActivationFunctionType

P = 128
B, C, D = 32, 128, 2048
NA, R = 8, 16
H, M = 16, 512
NS, HID = 8, 256
NK = D // P
GB = 4
GT = GB * C
NG = B // GB
HQ = 4
NQ = H // HQ
MT = M // P
KG = 7 * R
NIT = NQ * NG
STEPS = NIT * HQ
UNROLL = 8
LAST = STEPS // UNROLL
CREDIT = 1


def earlier(i, k, lag):
    i2, k2 = i + (k - lag) // UNROLL, (k - lag) % UNROLL
    if isinstance(i, int) and not 0 <= i2 < LAST:
        return None
    return i2, k2


def step_loop(engine, body, tail):
    for k in range(UNROLL):
        body(0, k)
    with engine.Fori(1, LAST) as i:
        for k in range(UNROLL):
            body(i, k)
    for k in range(tail):
        body(LAST, k)


def wait(engine, sem, count):
    if not (isinstance(count, int) and count <= 0):
        engine.wait_ge(sem, count)


def build(nc, xT, adown, bdown, up, down, w_sess, b_sess, w2, b2, qw, dense, perm, perm_row,
          adapter, session, chan_len, time_len, ident, expand, rows, out):
    with ExitStack() as top:
        def sem(name):
            return top.enter_context(nc.semaphore(name))

        def sb(ctx, name, shape, dt):
            return ctx.enter_context(nc.sbuf_tensor(name, shape, dt))

        g_dram = nc.dram_tensor("g_parts", [H, 3, R, NA, M], BF16).ap()
        bx_dram = nc.dram_tensor("bx_parts", [NG, P, GT], BF16).ap()
        ws_dram = nc.dram_tensor("ws_parts", [NS * C + 1, 2 * HID], F32).ap()
        dw_dram = nc.dram_tensor("down_parts", [H, P, 2 * MT * P], F32).ap()
        y_dram = nc.dram_tensor("y_rows", [NIT, P, HQ, GT], F32).ap()
        x1_dram = nc.dram_tensor("x1_rows", [NG * D, GT], F32).ap()

        ident_sb = sb(top, "ident_sb", [P, P], F32)
        rows_sb = sb(top, "rows_sb", [P, 2], F32)
        perm_sb = sb(top, "perm_sb", [P, NK], I32)
        shift = sb(top, "shift", [P, NK], I32)
        ysum = sb(top, "ysum", [P, STEPS], F32)
        dense_sb = sb(top, "dense_sb", [P, 3, NK], F32)
        nzero = sb(top, "nzero", [P, NK], F32)

        st01 = ExitStack()
        x_idx = sb(st01, "x_idx", [P, NIT, HQ], I32)
        w_idx = sb(st01, "w_idx", [P, NIT, GB], I32)
        ad_v = sb(st01, "ad_v", [P, NIT, GB], I32)
        time_f = sb(st01, "time_f", [P, B], F32)
        permrow_f = sb(st01, "permrow_f", [P, D], F32)
        bias_v = sb(st01, "bias_v", [P, 2, B], F32)
        b2_sb = sb(st01, "b2_sb", [P, 1], F32)
        w2h = sb(st01, "w2h", [P, 2, P], F32R)
        w2l = sb(st01, "w2l", [P, 2, P], F32R)
        dwt = sb(st01, "dwt", [P, HQ, 2, MT, P], F32R)
        gw = sb(st01, "gw", [P, HQ, NA, M], BF16)
        bxw = sb(st01, "bxw", [P, 2, GT], BF16)
        xt = sb(st01, "xt", [P, 2, HQ, GT], F32)

        psum = top.enter_context(nc.psum_tensor("psum", [P, 8, 512], F32))

        s_small = sem("small_loaded")
        s_tab = sem("tables_ready")
        s_up = sem("up_loaded")
        s_bld = sem("b_loaded")
        s_apg = sem("a_rows_loaded")
        s_acol = sem("a_tiles_picked")
        s_xc = [sem(f"x_chunk_loaded{c}") for c in range(4)]
        s_xcu = sem("x_chunk_used")
        s_draw = sem("down_loaded")
        s_gmm = sem("g_product")
        s_ghi = sem("g_high")
        s_gsp = sem("g_split")
        s_gst = sem("g_stored")
        s_bxe = sem("bx_copied")
        s_sel = sem("select_ready")
        s_bxs = sem("bx_selected")
        s_bsp = sem("bx_split")
        s_bst = sem("bx_stored")
        s_wsp = sem("w_split")
        s_wst = sem("w_stored")
        s_dhi = sem("down_high")
        s_dsp = sem("down_split")
        s_dst = sem("down_stored")
        s_dv = sem("vector_step")
        s_bmid = sem("bx_middle")
        s_tot = sem("y_totals")
        s_ph1 = sem("stage0_done")

        st0 = ExitStack()
        up_sb = sb(st0, "up_sb", [P, 2, M], F32)
        arow = sb(st0, "arow", [P, NK, P], F32)
        acol = sb(st0, "acol", [P, 2, P], F32)
        zrow = sb(st0, "zrow", [1, 2 * HID], F32)
        bcol = sb(st0, "bcol", [P, NK, P], F32)
        xch = sb(st0, "xch", [P, 4, 4, GT], F32)
        gpart = sb(st0, "gpart", [P, 3, 2, M], BF16)
        grest = sb(st0, "grest", [P, 2, M], F32)
        bx_sb = sb(st0, "bx_sb", [P, GT], F32)
        bxp = sb(st0, "bxp", [P, 3, GT], BF16)
        bxrest = sb(st0, "bxrest", [P, GT], F32)
        sel = sb(st0, "sel", [P, GB, P], F32)
        expand_sb = sb(st0, "expand_sb", [P, P], F32)
        amask = sb(st0, "amask", [P, B], F32)
        cmask = sb(st0, "cmask", [P, B], F32)
        w_row = sb(st0, "w_row", [P, 2, B], F32)
        wraw = sb(st0, "wraw", [P, NS, HID], F32)
        wsp = sb(st0, "wsp", [P, NS, 2, HID], F32R)
        draw = sb(st0, "draw", [P, 2, MT * P], F32)
        dsp = sb(st0, "dsp", [P, 2, 2, MT * P], F32R)
        w2raw = sb(st0, "w2raw", [P, 2, P], F32)
        ad_i = sb(st0, "ad_i", [P, B], I32)
        se_i = sb(st0, "se_i", [P, B], I32)
        cl_i = sb(st0, "cl_i", [P, B], I32)
        tl_i = sb(st0, "tl_i", [P, B], I32)
        pr_i = sb(st0, "pr_i", [P, D], I32)
        bs_sb = sb(st0, "bs_sb", [P, 2, NS], F32)
        seq = sb(st0, "seq", [P, NS, B], F32)
        pmod = sb(st0, "pmod", [P, NK], I32)
        st0.close()

        st1 = ExitStack()
        xch_ = sb(st1, "x1c_h", [P, 2, GB, HQ * P], F32R)
        xcl_ = sb(st1, "x1c_l", [P, 2, GB, HQ * P], F32R)
        ws = sb(st1, "ws", [P, 2, GB, 2, HID], F32R)
        raw = sb(st1, "act_raw", [P, 3, 2, 512], F32)
        ah = sb(st1, "act_h", [P, 2, 3, 2, 512], F32R)
        al = sb(st1, "act_l", [P, 2, 3, 2, 512], F32R)
        yb = sb(st1, "y_biased", [P, 512], F32)
        ym = sb(st1, "y_masked", [P, 512], F32)
        yt = sb(st1, "y_turned", [P, 2, HQ, P], F32)
        sx_idx = sb(st1, "step_x_idx", [P, 2, HQ], I32)
        sw_idx = sb(st1, "step_w_idx", [P, 2, GB], I32)
        st1.close()
        st01.close()

        U = [psum[:, 0:2, :], psum[:, 2:4, :]]
        DN, TX, YP, TY = (psum[:, b, :] for b in range(4, 8))

        s_gld = [sem(f"g_loaded{n}") for n in range(HQ)]
        s_bld1 = [sem(f"bx_loaded{n}") for n in range(2)]
        s_wld = [sem(f"w_loaded{n}") for n in range(2)]
        s_dld = [sem(f"down_parts_loaded{n}") for n in range(HQ)]
        s_xld = [sem(f"x_rows_loaded{n}") for n in range(2)]
        s_x1st = [sem(f"x1_rows_stored{n}") for n in range(2)]
        s_seen = sem("pool_waited")
        s_idx = sem("step_idx_ready")
        s_u = sem("hidden_product")
        s_gl = sem("gelu_done")
        s_gs = sem("gelu_split")
        s_dn = sem("down_product")
        s_x1 = sem("x1_ready")
        s_tx = sem("x1_turned")
        s_xh = sem("x1c_high")
        s_xl = sem("x1c_split")
        s_m1 = sem("mixer_product")
        s_gl1 = sem("mixer_gelu")
        s_gh1 = sem("mixer_high")
        s_gs1 = sem("mixer_split")
        s_m2 = sem("y_product")
        s_yb = sem("y_bias_added")
        s_ym = sem("y_mask_applied")
        s_ty = sem("y_turned_product")
        s_ye = sem("y_turned_copied")
        s_yst = [sem(f"y_stored{n}") for n in range(2)]

        st2 = ExitStack()
        q_sb = sb(st2, "q_sb", [P, NK, D], F32R)
        sum_sb = sb(st2, "sum_sb", [P, NG, GT], F32)
        yr = sb(st2, "yr", [P, 4, GT], F32)
        yh = sb(st2, "yh", [P, 4, GT], F32R)
        yl = sb(st2, "yl", [P, 4, GT], F32R)
        ones = sb(st2, "ones", [P, P], F32)
        sdiag = sb(st2, "sdiag", [P, 2, P], F32)
        ytot = sb(st2, "ytot", [P, B], F32)
        st2q = ExitStack()
        qraw = sb(st2q, "qraw", [P, 2, D], I32)
        st2q.close()
        dt_ = sb(st2, "dense_t", [P, 8, GT], F32)
        x1r = sb(st2, "x1r", [P, 4, GT], F32)
        st2.close()

        s_ph2 = sem("stage1_done")
        s_q = [sem(f"q_rows_loaded{n}") for n in range(2)]
        s_qb = sem("q_bits")
        s_qf = sem("q_ready")
        s_sd = sem("sum_diag")
        s_sm = sem("sum_product")
        s_se = sem("sum_copied")
        s_yld = [sem(f"y_loaded{n}") for n in range(4)]
        s_yh = sem("y_high")
        s_ysp = sem("y_split")
        s_yu = sem("y_used")
        s_x1l = [sem(f"x1_loaded{n}") for n in range(4)]
        s_acc = sem("dense_product")
        s_t = sem("zero_point_applied")
        s_du = sem("scale_applied")
        s_o = sem("out_ready")
        s_os = [sem(f"out_stored{n}") for n in range(8)]

        block = top.enter_context(nc.Block())
        SMALL = 16 * 14

        def wait_y_used(eng, g, half, k):
            hh = 2 * g + half
            if k >= 4:
                wait(eng, s_yu, hh * (NK - 1) + k - 3)
            elif not (isinstance(hh, int) and hh == 0):
                if k < 3:
                    eng.wait_ge(s_yu, (hh - 1) * (NK - 1) + k + NK - 3)
                else:
                    eng.wait_ge(s_acc, hh * 8)

        def enter_stage1(eng):
            eng.wait_ge(s_ph1, 4)

        @block.sync
        def _(sp):
            for dst, src in ((perm_sb, perm), (ad_i, adapter), (se_i, session), (cl_i, chan_len),
                             (tl_i, time_len), (rows_sb, rows), (ident_sb, ident),
                             (expand_sb, expand), (pr_i, perm_row), (b2_sb, b2)):
                sp.dma_start(dst[:], src[:]).then_inc(s_small, 16)
            sp.dma_start(bs_sb[:].rearrange("p a b -> p (a b)"), b_sess[:]).then_inc(s_small, 16)
            sp.dma_start(dense_sb[:].rearrange("p a b -> p (a b)"), dense[:]).then_inc(s_small, 16)
            sp.dma_start(w2raw[:].rearrange("p a b -> p (a b)"), w2[:]).then_inc(s_small, 16)
            sp.dma_start(wraw[:], w_sess[:].rearrange("(s c) h -> c s h", c=C)).then_inc(s_small, 16)
            sp.dma_start(bcol[:], bdown.rearrange("(k p) r -> p k r", p=P)).then_inc(s_bld, 16)

            def load_chunk(g, c):
                src = xT[bass.ds(g * D + c * 4 * P, 4 * P), :].rearrange("(k p) t -> p k t", p=P)
                sp.dma_start(xch[:, c, :, :], src).then_inc(s_xc[c], 16)

            def load_weights(g):
                sp.dma_start(up_sb[:].rearrange("p h m -> p (h m)"),
                             up[:, bass.ds(g * 2 * M, 2 * M)]).then_inc(s_up, 16)
                sp.dma_start(draw[:].rearrange("p a m -> p (a m)"),
                             down[:, bass.ds(g * 2 * MT * P, 2 * MT * P)]).then_inc(s_draw, 16)

            load_weights(0)
            for c in range(4):
                load_chunk(0, c)
            with sp.Fori(1, NG) as g:
                sp.wait_ge(s_gmm, g)
                sp.wait_ge(s_dsp, g)
                load_weights(g)
                for c in range(4):
                    sp.wait_ge(s_xcu, 4 * g - 3 + c)
                    load_chunk(g, c)

            def load_bx(g, par, free):
                g = g if isinstance(g, int) else sp.snap(g)
                wait(sp, s_u, free)
                sp.dma_start(bxw[:, par, :],
                             bx_dram[bass.ds(g, 1), :, :].rearrange("o p m -> (o p) m")).then_inc(s_bld1[par], 16)

            for q in range(NQ):
                for hq in range(HQ):
                    h = q * HQ + hq
                    wait(sp, s_u, 2 * (STEPS // NQ * q - HQ + 1 + hq) if q else 0)
                    if h % 2 == 0:
                        sp.wait_ge(s_gst, 48 * (h // 2 + 1))
                        sp.wait_ge(s_dst, 16 * (h // 2 + 1))
                    for rep in range(4):
                        parts, lo, n = ((0, 2), 2 * R * rep, 2 * R) if rep < 3 else ((2, 3), 6 * R, R)
                        sp.dma_start(gw[lo:lo + n, hq, :, :].rearrange("p a m -> p (a m)"),
                                     g_dram[h, parts[0]:parts[1], :, :, :].rearrange("x r a m -> (x r) (a m)")).then_inc(s_gld[hq], 16)
                    wait(sp, s_dn, (STEPS // NQ * q - HQ + 1 + hq) if q else 0)
                    sp.dma_start(dwt[:, hq, :, :, :].rearrange("p x m d -> p (x m d)").bitcast(F32),
                                 dw_dram[h, :, :]).then_inc(s_dld[hq], 16)

                def iteration(j, par):
                    it = NG * q + 2 * j + par
                    if not (isinstance(j, int) and it == NIT - 1):
                        load_bx((2 * j + par + 1) % NG, 1 - par, 2 * HQ * it)

                if q == 0:
                    sp.wait_ge(s_bst, 64 * NG)
                    load_bx(0, 0, 0)
                iteration(0, 0)
                iteration(0, 1)
                with sp.Fori(1, NG // 2 - 1) as j:
                    iteration(j, 0)
                    iteration(j, 1)
                iteration(NG // 2 - 1, 0)
                iteration(NG // 2 - 1, 1)

            sp.wait_ge(s_ph2, 4)

            def load_half(g, half):
                for k in range(NK):
                    n = k % 4
                    it = g + NG * (k // HQ)
                    it = it if isinstance(it, int) else sp.snap(it)
                    wait(sp, s_ysp, (2 * g + half) * NK + k - 3)
                    sp.dma_start(yr[:, n, :],
                                 y_dram[bass.ds(it, 1), :, k % HQ, :].rearrange("o p t -> (o p) t")).then_inc(s_yld[n], 16)
                    if 6 <= k < 14 and not (isinstance(g, int) and g == 0 and half == 0):
                        load_x1(g, half, k - 6)

            def load_x1(g, half, n):
                row = g * D + (half - 1) * 8 * P + n * P
                row = row if isinstance(row, int) else sp.snap(row)
                if n == 0 and isinstance(g, int):
                    sp.wait_ge(s_qf, NK)
                wait(sp, s_o, (2 * g + half - 1) * 8 + n - 3)
                sp.dma_start(x1r[:, n % 4, :], x1_dram[bass.ds(row, P), :]).then_inc(s_x1l[n % 4], 16)

            load_half(0, 0)
            load_half(0, 1)
            with sp.Fori(1, NG) as g:
                load_half(g, 0)
                load_half(g, 1)
            for n in range(8):
                load_x1(NG, 0, n)
            for n in range(8):
                sp.wait_ge(s_os[n], 16 * NG * 2)

        @block.gpsimd
        def _(pool):
            pool.wait_ge(s_small, SMALL)
            for k in range(NK):
                nc.gpsimd.indirect_dma_start(
                    arow[:, k, :], None, adown[:],
                    bass.IndirectOffsetOnAxis(ap=perm_sb[:, k:k + 1], axis=0)).then_inc(s_apg, 16)
            pool.wait_ge(s_apg, 16 * NK)
            pool.wait_ge(s_tab, 1)

            def gather_x(it, par, n):
                nc.gpsimd.tensor_copy(sx_idx[:, par, :], x_idx[:, bass.ds(it, 1), :].rearrange("p o h -> p (o h)")).then_inc(s_idx, 1)
                pool.wait_ge(s_idx, n)
                pool.sem_inc(s_seen, 1)
                for hq in range(HQ):
                    nc.gpsimd.indirect_dma_start(
                        xt[:, par, hq, :], None, xT[:],
                        bass.IndirectOffsetOnAxis(ap=sx_idx[:, par, hq:hq + 1], axis=0)).then_inc(s_xld[par], 16)

            def gather_w(it, par, n):
                nc.gpsimd.tensor_copy(sw_idx[:, par, :], w_idx[:, bass.ds(it, 1), :].rearrange("p o h -> p (o h)")).then_inc(s_idx, 1)
                pool.wait_ge(s_idx, n)
                pool.sem_inc(s_seen, 1)
                for b in range(GB):
                    nc.gpsimd.indirect_dma_start(
                        ws[:, par, b, :, :].rearrange("p x h -> p (x h)").bitcast(F32), None, ws_dram[:],
                        bass.IndirectOffsetOnAxis(ap=sw_idx[:, par, b:b + 1], axis=0)).then_inc(s_wld[par], 16)

            def scatter_x1(it, par):
                for hq in range(HQ):
                    pool.wait_ge(s_x1, HQ * it + hq + 1)
                    pool.sem_inc(s_seen, 1)
                    nc.gpsimd.indirect_dma_start(
                        x1_dram[:], bass.IndirectOffsetOnAxis(ap=sx_idx[:, par, hq:hq + 1], axis=0),
                        xt[:, par, hq, :], None).then_inc(s_x1st[par], 16)

            pool.sem_inc(s_ph1, 1)
            gather_x(0, 0, 1)
            gather_x(1, 1, 2)
            enter_stage1(pool)
            pool.wait_ge(s_wst, 32)
            gather_w(0, 0, 3)

            def iteration(it, par, first):
                scatter_x1(it, par)
                if not (isinstance(it, int) and it >= NIT - 2):
                    pool.wait_ge(s_tx, HQ * (it + 1))
                    pool.wait_ge(s_x1st[par], 16 * HQ * (first + 1))
                    pool.sem_inc(s_seen, 1)
                    gather_x(it + 2, par, 2 * it + 4)
                if not (isinstance(it, int) and it == NIT - 1):
                    wait(pool, s_m1, HQ * it)
                    pool.sem_inc(s_seen, 1)
                    gather_w(it + 1, 1 - par, 2 * it + 5 if not (isinstance(it, int) and it >= NIT - 2) else 2 * NIT)

            iteration(0, 0, 0)
            iteration(1, 1, 0)
            with pool.Fori(1, NIT // 2 - 1) as j:
                iteration(2 * j, 0, j)
                iteration(2 * j + 1, 1, j)
            iteration(NIT - 2, 0, 0)
            iteration(NIT - 1, 1, 0)
            for par in range(2):
                pool.wait_ge(s_x1st[par], 16 * HQ * NIT // 2)
            pool.sem_inc(s_ph2, 1)
            pool.wait_ge(s_ph2, 4)
            for k in range(NK):
                wait(pool, s_qf, k - 1)
                nc.gpsimd.indirect_dma_start(
                    qraw[:, k % 2, :], None, qw[:],
                    bass.IndirectOffsetOnAxis(ap=perm_sb[:, k:k + 1], axis=0)).then_inc(s_q[k % 2], 16)
            with pool.Fori(0, 2 * NG) as hh:
                for n in range(8):
                    row = pool.snap(hh * 8 * P + n * P)
                    pool.wait_ge(s_o, hh * 8 + n + 1)
                    pool.sem_inc(s_seen, 1)
                    pool.dma_start(out[bass.ds(row, P), :], dt_[:, n, :]).then_inc(s_os[n], 16)

        @block.tensor
        def _(pe):
            pe.wait_ge(s_bld, 16)

            def adapter_rows(g):
                pe.wait_ge(s_up, 16 * g + 16)
                pe.wait_ge(s_acol, g + 1)
                wait(pe, s_gsp, g)
                for n in range(2):
                    mm = nc.tensor.matmul(psum[:, n, :], acol[:, n, :], up_sb[:, n, :], start=True, stop=True)
                mm.then_inc(s_gmm, 1)
                wait(pe, s_bxe, g)
                for k in range(NK):
                    if k % 4 == 0:
                        pe.wait_ge(s_xc[k // 4], 16 * g + 16)
                    mm = nc.tensor.matmul(psum[:, 2, :], bcol[:, k, :], xch[:, k // 4, k % 4, :],
                                          start=(k == 0), stop=(k == NK - 1))
                    if k % 4 == 3:
                        mm.then_inc(s_xcu, 1)
                pe.wait_ge(s_bxe, g + 1)
                pe.wait_ge(s_sel, g + 1)
                wait(pe, s_bsp, g)
                for b in range(GB):
                    mm = nc.tensor.matmul(psum[:, 3, b * C:(b + 1) * C], sel[:, b, :],
                                          bx_sb[:, b * C:(b + 1) * C], start=True, stop=True)
                mm.then_inc(s_bxs, 1)

            adapter_rows(0)
            with pe.Fori(1, NG) as g:
                adapter_rows(g)
            pe.wait_ge(s_bsp, NG)
            pe.sem_inc(s_ph1, 1)
            enter_stage1(pe)

            adapters = ad_v[0:1, :, :].rearrange("p i b -> p (i b)")
            chosen = [None] * GB

            def hidden(i, k, part):
                u = U[(k + part) % 2]
                for m in range(2):
                    for b in range(GB):
                        col = (2 * part + m) * P
                        g_tile = gw[0:KG, k % HQ, bass.ds(chosen[b], 1), col:col + P].rearrange("p o m -> p (o m)")
                        mm = nc.tensor.matmul(u[:, m, b * C:(b + 1) * C], g_tile,
                                              bxw[0:KG, k // HQ, b * C:(b + 1) * C], start=True, stop=True)
                mm.then_inc(s_u, 1)

            def step(i, k):
                s = UNROLL * i + k
                now, dn, tx = earlier(i, k, 0), earlier(i, k, 1), earlier(i, k, 2)
                m1, m2, ty = earlier(i, k, 6), earlier(i, k, 7), earlier(i, k, 8)
                if now:
                    if k % HQ == 0:
                        for b in range(GB):
                            col = (2 * i + k // HQ) * GB + b
                            chosen[b] = pe.value_load(adapters[:, bass.ds(col, 1)], min_val=0, max_val=NA - 1)
                        pe.wait_ge(s_bld1[k // HQ], 16 * (i + 1))
                    if k < HQ:
                        pe.wait_ge(s_gld[k], 64 * (i // (NG // 2) + 1))
                    wait(pe, s_gl, 2 * s)
                    hidden(i, k, 0)
                if tx:
                    j = UNROLL * tx[0] + tx[1]
                    pe.wait_ge(s_x1, j + 1)
                    wait(pe, s_xl, j)
                    for b in range(GB):
                        mm = nc.tensor.transpose(TX[:, b * C:(b + 1) * C],
                                                 xt[:, tx[1] // HQ, tx[1] % HQ, b * C:(b + 1) * C], ident_sb[:])
                    mm.then_inc(s_tx, 1)
                if now:
                    if earlier(i, k, 7):
                        pe.wait_ge(s_gl1, s - 6)
                    hidden(i, k, 1)
                if dn:
                    j = UNROLL * dn[0] + dn[1]
                    par, hq = dn[1] // HQ, dn[1] % HQ
                    if par == 0:
                        pe.wait_ge(s_dld[hq], 16 * (dn[0] // (NG // 2) + 1))
                    pe.wait_ge(s_gs, 2 * j + 2)
                    wait(pe, s_x1, j)
                    n = 0
                    for m in range(MT):
                        for w, a in ((0, ah), (1, ah), (0, al)):
                            mm = nc.tensor.matmul(DN, dwt[:, hq, w, m, :], a[:, dn[1] % 2, m // 2, m % 2, :],
                                                  start=(n == 0), stop=(n == 3 * MT - 1))
                            n += 1
                    mm.then_inc(s_dn, 1)
                if ty:
                    v = UNROLL * ty[0] + ty[1]
                    pe.wait_ge(s_ym, v + 1)
                    wait(pe, s_ye, v + CREDIT)
                    for t in range(HQ):
                        mm = nc.tensor.transpose(TY[:, t * P:(t + 1) * P], ym[:, t * P:(t + 1) * P], ident_sb[:])
                    mm.then_inc(s_ty, 1)
                if m1:
                    v = UNROLL * m1[0] + m1[1]
                    par, b = m1[1] // GB, m1[1] % GB
                    if b == 0:
                        pe.wait_ge(s_wld[par], 16 * GB * (m1[0] + 1))
                        pe.wait_ge(s_xl, v + GB)
                    if now:
                        pe.wait_ge(s_gl, 2 * s + 1)
                    else:
                        pe.wait_ge(s_gl, 2 * STEPS)
                        pe.wait_ge(s_gl1, v - 1)
                    u = U[k % 2]
                    for x in range(2):
                        n = 0
                        for w, a in ((0, xch_), (1, xch_), (0, xcl_)):
                            mm = nc.tensor.matmul(u[:, x, :], ws[:, par, b, w, x * P:(x + 1) * P],
                                                  a[:, par, b, :], start=(n == 0), stop=(n == 2))
                            n += 1
                    mm.then_inc(s_m1, 1)
                if m2:
                    v = UNROLL * m2[0] + m2[1]
                    pe.wait_ge(s_gs1, v + 1)
                    wait(pe, s_yb, v)
                    n = 0
                    for x in range(2):
                        for w, a in ((w2h, ah), (w2l, ah), (w2h, al)):
                            mm = nc.tensor.matmul(YP, w[:, x, :], a[:, m2[1] % 2, 2, x, :],
                                                  start=(n == 0), stop=(n == 5))
                            n += 1
                    mm.then_inc(s_m2, 1)

            pe.sem_inc(s_m2, CREDIT)
            step_loop(pe, step, 8)
            pe.sem_inc(s_ph2, 1)
            pe.wait_ge(s_ph2, 4)

            for b in range(B):
                pe.wait_ge(s_sd, b + 2)
                bank = b // GB
                mm = nc.tensor.matmul(psum[:, bank, b % GB * C:(b % GB + 1) * C], ones[:], sdiag[:, b % 2, :],
                                      start=True, stop=True)
                mm.then_inc(s_sm, 1)

            def dense_group(g):
                for half in range(2):
                    for k in range(NK):
                        pe.wait_ge(s_qf, k + 1)
                        pe.wait_ge(s_ysp, g * 2 * NK + half * NK + k + 1)
                        for n in range(8):
                            if k == 0:
                                if half == 0 and isinstance(g, int):
                                    pe.wait_ge(s_se, n + 1)
                                else:
                                    pe.wait_ge(s_t, g * NK + half * 8 + n - 7)
                            col = (half * 8 + n) * P
                            nc.tensor.matmul(psum[:, n, :], q_sb[:, k, col:col + P], yh[:, k % 4, :],
                                             start=(k == 0), stop=False)
                            mm = nc.tensor.matmul(psum[:, n, :], q_sb[:, k, col:col + P], yl[:, k % 4, :],
                                                  start=False, stop=(k == NK - 1))
                            if k == NK - 1:
                                mm.then_inc(s_acc, 1)
                            elif n == 7:
                                mm.then_inc(s_yu, 1)
            dense_group(0)
            with pe.Fori(1, NG) as g:
                dense_group(g)

        @block.scalar
        def _(act):
            act.wait_ge(s_wsp, 1)
            act.dma_start(ws_dram[0:NS * C, :].rearrange("(s c) h -> c s h", c=C),
                          wsp[:].rearrange("p s x h -> p s (x h)").bitcast(F32)).then_inc(s_wst, 16)
            act.dma_start(ws_dram[NS * C:NS * C + 1, :], zrow[:]).then_inc(s_wst, 16)

            def prepare(g):
                act.wait_ge(s_gmm, g + 1)
                wait(act, s_gst, 48 * g)
                nc.scalar.activation(gpart[:, 0, :, :], psum[:, 0:2, :], ACT.Copy).then_inc(s_ghi, 1)
                act.wait_ge(s_draw, 16 * g + 16)
                wait(act, s_dst, 16 * g)
                nc.scalar.activation(dsp[:, :, 0, :], draw[:], ACT.Copy).then_inc(s_dhi, 1)
                act.wait_ge(s_gsp, g + 1)
                for part in range(3):
                    act.dma_start(g_dram[bass.ds(2 * g, 2), part, :, :, :].rearrange("h r a m -> (r a) h m"),
                                  gpart[:, part, :, :]).then_inc(s_gst, 16)
                act.wait_ge(s_dsp, g + 1)
                act.dma_start(dw_dram[bass.ds(2 * g, 2), :, :].rearrange("h p x -> p h x"),
                              dsp[:].rearrange("p h x m -> p h (x m)").bitcast(F32)).then_inc(s_dst, 16)
                act.wait_ge(s_xcu, 4 * g + 4)
                wait(act, s_bxs, g)
                nc.scalar.activation(bx_sb[:], psum[:, 2, :], ACT.Copy).then_inc(s_bxe, 1)
                act.wait_ge(s_bsp, g + 1)
                for lo, part in ((0, 0), (32, 1), (64, 2), (96, 0)):
                    act.dma_start(bx_dram[bass.ds(g, 1), lo:lo + 32, :].rearrange("o p t -> (o p) t"),
                                  bxp[lo:lo + 32, part, :]).then_inc(s_bst, 16)

            prepare(0)
            with act.Fori(1, NG) as g:
                prepare(g)
            act.wait_ge(s_wst, 32)
            act.wait_ge(s_gst, 48 * NG)
            act.wait_ge(s_bst, 64 * NG)
            act.wait_ge(s_dst, 16 * NG)
            act.sem_inc(s_ph1, 1)
            enter_stage1(act)

            def gelu(i, k, part):
                s = UNROLL * i + k
                wait(act, s_dn, s - 1)
                nc.scalar.activation(ah[:, k % 2, part, :, :], U[(k + part) % 2], ACT.Gelu)
                wait(act, s_gs, 2 * s - 1 + part)
                nc.scalar.activation(raw[:, part, :, :], U[(k + part) % 2], ACT.Gelu).then_inc(s_gl, 1)

            def step(i, k):
                s = UNROLL * i + k
                now, tx = earlier(i, k, 0), earlier(i, k, 2)
                m1, m2, ty = earlier(i, k, 6), earlier(i, k, 7), earlier(i, k, 8)
                if now:
                    act.wait_ge(s_u, 2 * s + 1)
                    gelu(i, k, 0)
                if tx:
                    j = UNROLL * tx[0] + tx[1]
                    act.wait_ge(s_tx, j + 1)
                    if tx[1] % HQ == 0:
                        wait(act, s_m1, j - HQ)
                    dst = xch_[:, tx[1] // HQ, :, tx[1] % HQ * P:(tx[1] % HQ + 1) * P]
                    nc.scalar.activation(dst, TX.rearrange("p (b t) -> p b t", b=GB), ACT.Copy).then_inc(s_xh, 1)
                if now:
                    act.wait_ge(s_u, 2 * s + 2)
                    gelu(i, k, 1)
                if ty:
                    v = UNROLL * ty[0] + ty[1]
                    act.wait_ge(s_ty, v + 1)
                    wait(act, s_yst[k % 2], 8 * (v - ty[1] % 2) + CREDIT)
                    nc.scalar.activation(yt[:, k % 2, :, :].rearrange("p a b -> p (a b)"), TY, ACT.Copy).then_inc(s_ye, 1)
                if m1:
                    v = UNROLL * m1[0] + m1[1]
                    act.wait_ge(s_m1, v + 1)
                    wait(act, s_gs1, v)
                    b = UNROLL * (m1[0] % (NG // 2)) + m1[1]
                    for x in range(2):
                        a = nc.scalar.activation(raw[:, 2, x, :], U[k % 2][:, x, :], ACT.Gelu,
                                                 bias=bias_v[:, x, bass.ds(b, 1)])
                    a.then_inc(s_gl1, 1)
                if ty:
                    act.wait_ge(s_ye, UNROLL * ty[0] + ty[1] + 1 + CREDIT)
                    y_dst = y_dram[bass.ds(2 * ty[0] + ty[1] // GB, 1), :, :, ty[1] % GB * C:(ty[1] % GB + 1) * C]
                    act.dma_start(y_dst.rearrange("o p k t -> (o p) k t"), yt[:, k % 2, :, :]).then_inc(s_yst[k % 2], 16)
                if m2:
                    v = UNROLL * m2[0] + m2[1]
                    act.wait_ge(s_m2, v + 1 + CREDIT)
                    wait(act, s_ym, v)
                    nc.scalar.activation(yb[:], YP, ACT.Identity, bias=b2_sb[:, 0:1]).then_inc(s_yb, 1)

            act.sem_inc(s_ye, CREDIT)
            for n in range(2):
                act.sem_inc(s_yst[n], CREDIT)
            step_loop(act, step, 8)
            for n in range(2):
                act.wait_ge(s_yst[n], 8 * STEPS + CREDIT)
            act.sem_inc(s_ph2, 1)
            act.wait_ge(s_ph2, 4)

            for bank in range(NG):
                act.wait_ge(s_sm, GB * (bank + 1))
                nc.scalar.activation(sum_sb[:, bank, :], psum[:, bank, :], ACT.Copy).then_inc(s_se, 1)

            def unpack(k):
                act.wait_ge(s_qb, k + 1)
                nc.scalar.activation(q_sb[:, k, :], qraw[:, k % 2, :], ACT.Copy).then_inc(s_qf, 1)

            def y_high(g, half, k):
                act.wait_ge(s_yld[k % 4], 16 * (8 * g + 4 * half + k // 4 + 1))
                wait_y_used(act, g, half, k)
                nc.scalar.activation(yh[:, k % 4, :], yr[:, k % 4, :], ACT.Copy).then_inc(s_yh, 1)

            def scale(g, half):
                for n in range(8):
                    nn = 8 * (1 - half) + n
                    act.wait_ge(s_t, (2 * g + half - 1) * 8 + n + 1)
                    nc.scalar.activation(dt_[:, n, :], dt_[:, n, :], ACT.Identity, bias=dense_sb[:, 2, nn:nn + 1],
                                         scale=dense_sb[:, 0, nn:nn + 1]).then_inc(s_du, 1)

            def half_group(g, half):
                for k in range(3):
                    y_high(g, half, k)
                scale(g, half)
                for k in range(3, NK):
                    y_high(g, half, k)

            unpack(0)
            for k in range(NK):
                if k + 1 < NK:
                    unpack(k + 1)
                y_high(0, 0, k)
            half_group(0, 1)
            with act.Fori(1, NG) as g:
                half_group(g, 0)
                half_group(g, 1)
            scale(NG, 0)

        @block.vector
        def _(dve):
            done = 0

            def own(instruction):
                nonlocal done
                done += 1
                instruction.then_inc(s_dv, 1)

            def after_own():
                dve.wait_ge(s_dv, done)

            dve.wait_ge(s_small, SMALL)
            v = nc.vector
            for g in range(NG):
                own(v.tensor_scalar(x_idx[:, :, :].rearrange("p (q g) h -> p q g h", g=NG)[:, :, g, :],
                                    perm_sb[:].rearrange("p (q h) -> p q h", h=HQ), g * D, None, ALU.add))
            for q in range(NQ):
                own(v.tensor_copy(ad_v[:, q * NG:(q + 1) * NG, :].rearrange("p g b -> p (g b)"), ad_i[:]))
            own(v.tensor_scalar(w_row[:, 0, :], se_i[:], C, rows_sb[:, 0:1], ALU.mult, ALU.add))
            own(v.tensor_scalar(amask[:], ad_i[:], rows_sb[:, 1:2], None, ALU.is_equal))
            own(v.tensor_scalar(cmask[:], cl_i[:], rows_sb[:, 0:1], None, ALU.is_gt))
            own(v.memset(zrow[:], 0.0))
            own(v.tensor_copy(wsp[:, :, 0, :], wraw[:]))
            own(v.tensor_copy(time_f[:], tl_i[:]))
            own(v.tensor_copy(permrow_f[:], pr_i[:]))
            own(v.tensor_scalar(nzero[:], dense_sb[:, 1, :], -1.0, None, ALU.mult))
            own(v.tensor_scalar(pmod[:], perm_sb[:], 3, None, ALU.bitwise_and))
            own(v.memset(bias_v[:], 0.0))
            for n in range(NS):
                own(v.tensor_scalar(seq[:, n, :], se_i[:], n, None, ALU.is_equal))
            own(v.tensor_copy(w2h[:], w2raw[:]))
            after_own()
            own(v.tensor_scalar(shift[:], pmod[:], 1, 6, ALU.is_equal, ALU.mult))
            own(v.tensor_tensor(w2l[:], w2raw[:], w2h[:].bitcast(F32), ALU.subtract))
            v.tensor_tensor(wsp[:, :, 1, :], wraw[:], wsp[:, :, 0, :].bitcast(F32), ALU.subtract).then_inc(s_wsp, 1)
            own(v.scalar_tensor_tensor(w_row[:, 1, :], w_row[:, 0, :], float(-NS * C), cmask[:], ALU.add, ALU.mult))
            after_own()
            for q in range(NQ):
                own(v.tensor_scalar(w_idx[:, q * NG:(q + 1) * NG, :].rearrange("p g b -> p (g b)"),
                                    w_row[:, 1, :], float(NS * C), None, ALU.add))
            for n in range(NS):
                for x in range(2):
                    own(v.scalar_tensor_tensor(bias_v[:, x, :], seq[:, n, :], bs_sb[:, x, n:n + 1],
                                               bias_v[:, x, :], ALU.mult, ALU.add))
                after_own()
            v.tensor_copy(seq[:, 0, :], seq[:, 1, :]).then_inc(s_tab, 1)

            dve.wait_ge(s_tab, 1)
            dve.wait_ge(s_apg, 16 * NK)
            base = done

            def prepare(g):
                wait(dve, s_gmm, g)
                v.tensor_copy(acol[:], arow[:, bass.ds(2 * g, 2), :]).then_inc(s_acol, 1)
                wait(dve, s_bxs, g)
                for b in range(GB):
                    a = v.tensor_scalar(sel[:, b, :], expand_sb[:], amask[:, bass.ds(g * GB + b, 1)], None, ALU.mult)
                a.then_inc(s_sel, 1)
                dve.wait_ge(s_ghi, g + 1)
                v.tensor_tensor(grest[:], psum[:, 0:2, :], gpart[:, 0, :, :], ALU.subtract).then_inc(s_dv, 1)
                dve.wait_ge(s_dv, 4 * g + (base + 1))
                v.tensor_copy(gpart[:, 1, :, :], grest[:]).then_inc(s_dv, 1)
                dve.wait_ge(s_dv, 4 * g + (base + 2))
                v.tensor_tensor(gpart[:, 2, :, :], grest[:], gpart[:, 1, :, :], ALU.subtract).then_inc(s_gsp, 1)
                dve.wait_ge(s_gsp, g + 1)
                dve.wait_ge(s_dhi, g + 1)
                v.tensor_tensor(dsp[:, :, 1, :], draw[:], dsp[:, :, 0, :].bitcast(F32), ALU.subtract).then_inc(s_dsp, 1)
                dve.wait_ge(s_bxs, g + 1)
                wait(dve, s_bst, 64 * g)
                v.tensor_copy(bxp[:, 0, :], psum[:, 3, :]).then_inc(s_dv, 1)
                dve.wait_ge(s_dv, 4 * g + (base + 3))
                v.tensor_tensor(bxrest[:], psum[:, 3, :], bxp[:, 0, :], ALU.subtract).then_inc(s_dv, 1)
                dve.wait_ge(s_dv, 4 * g + (base + 4))
                v.tensor_copy(bxp[:, 1, :], bxrest[:]).then_inc(s_bmid, 1)
                dve.wait_ge(s_bmid, g + 1)
                v.tensor_tensor(bxp[:, 2, :], bxrest[:], bxp[:, 1, :], ALU.subtract).then_inc(s_bsp, 1)
                dve.wait_ge(s_bsp, g + 1)

            prepare(0)
            with dve.Fori(1, NG) as g:
                prepare(g)
            dve.wait_ge(s_wsp, 1)
            dve.wait_ge(s_dsp, NG)
            dve.sem_inc(s_ph1, 1)
            enter_stage1(dve)

            def low(par, slot, done_sem):
                v.tensor_tensor(al[:, par, slot, :, :], raw[:, slot, :, :],
                                ah[:, par, slot, :, :].bitcast(F32), ALU.subtract).then_inc(done_sem, 1)

            def step(i, k):
                s = UNROLL * i + k
                now, dn, tx = earlier(i, k, 0), earlier(i, k, 1), earlier(i, k, 2)
                m2, ym_item = earlier(i, k, 7), earlier(i, k, 8)
                if m2:
                    v2 = UNROLL * m2[0] + m2[1]
                    dve.wait_ge(s_gl1, v2 + 1)
                    wait(dve, s_m2, v2 - 1 + CREDIT)
                    v.tensor_copy(ah[:, m2[1] % 2, 2, :, :], raw[:, 2, :, :]).then_inc(s_gh1, 1)
                    dve.wait_ge(s_gh1, v2 + 1)
                    low(m2[1] % 2, 2, s_gs1)
                if ym_item:
                    v3 = UNROLL * ym_item[0] + ym_item[1]
                    dve.wait_ge(s_yb, v3 + 1)
                    wait(dve, s_ty, v3)
                    b = UNROLL * (ym_item[0] % (NG // 2)) + ym_item[1]
                    v.scalar_tensor_tensor(ym[:], permrow_f[:, bass.ds(ym_item[0] // (NG // 2) * HQ * P, HQ * P)],
                                           time_f[:, bass.ds(b, 1)], yb[:], ALU.is_lt, ALU.mult,
                                           accum_out=ysum[:, bass.ds(v3, 1)]).then_inc(s_ym, 1)
                if now:
                    dve.wait_ge(s_gl, 2 * s + 1)
                    wait(dve, s_dn, s - 1)
                    low(k % 2, 0, s_gs)
                if tx:
                    j = UNROLL * tx[0] + tx[1]
                    dve.wait_ge(s_xh, j + 1)
                    cols = slice(tx[1] % HQ * P, (tx[1] % HQ + 1) * P)
                    par = tx[1] // HQ
                    v.tensor_tensor(xcl_[:, par, :, cols], TX.rearrange("p (b t) -> p b t", b=GB),
                                    xch_[:, par, :, cols].bitcast(F32), ALU.subtract).then_inc(s_xl, 1)
                if now:
                    dve.wait_ge(s_gl, 2 * s + 2)
                    low(k % 2, 1, s_gs)
                if dn:
                    j = UNROLL * dn[0] + dn[1]
                    par, hq = dn[1] // HQ, dn[1] % HQ
                    dve.wait_ge(s_dn, j + 1)
                    dve.wait_ge(s_xld[par], 16 * HQ * (dn[0] + 1))
                    v.tensor_tensor(xt[:, par, hq, :], xt[:, par, hq, :], DN, ALU.add).then_inc(s_x1, 1)

            step_loop(dve, step, 8)
            for watched, count in ((s_x1, STEPS), (s_ym, STEPS), (s_xl, STEPS), (s_gs1, STEPS)):
                dve.wait_ge(watched, count)
            dve.sem_inc(s_ph2, 1)
            dve.wait_ge(s_ph2, 4)

            v.memset(ones[:], 1.0).then_inc(s_sd, 1)
            n_tot = 0
            ys = ysum[:].rearrange("p (q b) -> p q b", b=B)
            for a, b in ((ys[:, 0, :], ys[:, 1, :]), (ytot[:], ys[:, 2, :]), (ytot[:], ys[:, 3, :])):
                v.tensor_tensor(ytot[:], a, b, ALU.add).then_inc(s_tot, 1)
                n_tot += 1
                dve.wait_ge(s_tot, n_tot)
            for b in range(B):
                wait(dve, s_sm, b - 1)
                v.tensor_scalar(sdiag[:, b % 2, :], ident_sb[:], ytot[:, b:b + 1], None, ALU.mult).then_inc(s_sd, 1)

            def bits(k):
                dve.wait_ge(s_q[k % 2], 16 * (k // 2 + 1))
                v.tensor_scalar(qraw[:, k % 2, :], qraw[:, k % 2, :], shift[:, k:k + 1], 63,
                                ALU.logical_shift_right, ALU.bitwise_and).then_inc(s_qb, 1)

            def y_low(g, half, k):
                dve.wait_ge(s_yh, (2 * g + half) * NK + k + 1)
                v.tensor_tensor(yl[:, k % 4, :], yr[:, k % 4, :], yh[:, k % 4, :].bitcast(F32),
                                ALU.subtract).then_inc(s_ysp, 1)

            def zero_point(g, half):
                last_g = g - 1 if half == 0 else g
                for n in range(8):
                    nn = 8 * (1 - half) + n
                    dve.wait_ge(s_acc, (2 * g + half - 1) * 8 + n + 1)
                    wait(dve, s_os[n], 16 * (2 * g + half - 1))
                    v.scalar_tensor_tensor(dt_[:, n, :], sum_sb[:, bass.ds(last_g, 1), :].rearrange("p o t -> p (o t)"),
                                           nzero[:, nn:nn + 1], psum[:, n, :], ALU.mult, ALU.add).then_inc(s_t, 1)

            def add_x1(g, half, n):
                e = (2 * g + half - 1) * 8 + n
                dve.wait_ge(s_du, e + 1)
                dve.wait_ge(s_x1l[n % 4], 16 * (2 * (2 * g + half - 1) + n // 4 + 1))
                v.tensor_tensor(dt_[:, n, :], dt_[:, n, :], x1r[:, n % 4, :], ALU.add).then_inc(s_o, 1)

            def half_group(g, half):
                for k in range(3):
                    y_low(g, half, k)
                zero_point(g, half)
                for k in range(3, NK):
                    y_low(g, half, k)
                    if 5 <= k < 13:
                        add_x1(g, half, k - 5)

            bits(0)
            for k in range(NK):
                if k + 1 < NK:
                    bits(k + 1)
                y_low(0, 0, k)
            half_group(0, 1)
            with dve.Fori(1, NG) as g:
                half_group(g, 0)
                half_group(g, 1)
            zero_point(NG, 0)
            for n in range(8):
                add_x1(NG, 0, n)


def kernel(x, itok_B_3_7, itok_B_0_7, itok_B_2182_4065, _lenS, L0_cond_A, L0_cond_B, L0_ffn_up, L0_ffn_down,
           L0_ffn_perm, L1_cond_W_sess, L1_cond_b_sess, L1_cond_W2, L1_cond_b2, L1_ffn_qweight,
           L1_ffn_weight_scale, L1_ffn_weight_zero_point, L1_ffn_bias):
    import concourse.bacc as bacc
    from concourse.bass_utils import run_bass_kernel_spmd

    def spread(a):
        a = np.asarray(a)
        return np.ascontiguousarray(np.broadcast_to(a[None, :], (P, a.shape[0])))

    def columns(a):
        return np.asarray(a).reshape(NK, P).T

    k = np.arange(D)
    word = 3 * (k // 4) + np.array([0, 0, 1, 2])[k % 4]
    p = np.arange(P)
    arrays = {
        "xT": np.asarray(x).reshape(NG, GT, D).transpose(0, 2, 1).reshape(NG * D, GT),
        "adown": np.asarray(L0_cond_A).transpose(1, 2, 0).reshape(D, R * NA),
        "bdown": np.asarray(L0_cond_B).transpose(2, 1, 0).reshape(D, R * NA),
        "up": np.asarray(L0_ffn_up).transpose(1, 0, 2).reshape(P, H * M),
        "down": np.asarray(L0_ffn_down).reshape(H, MT, P, P).transpose(2, 0, 1, 3).reshape(P, H * MT * P),
        "w_sess": np.asarray(L1_cond_W_sess).reshape(NS * C, HID),
        "b_sess": np.asarray(L1_cond_b_sess).reshape(NS, 2, P).transpose(2, 1, 0).reshape(P, 2 * NS),
        "w2": np.asarray(L1_cond_W2).reshape(2, P, P).transpose(1, 0, 2).reshape(P, 2 * P),
        "b2": np.asarray(L1_cond_b2).reshape(P, 1),
        "qw": np.asarray(L1_ffn_qweight).T[word],
        "dense": np.stack([columns(L1_ffn_weight_scale), columns(L1_ffn_weight_zero_point),
                           columns(L1_ffn_bias)], axis=1).reshape(P, 3 * NK),
        "perm": columns(L0_ffn_perm),
        "perm_row": spread(L0_ffn_perm),
        "adapter": spread(itok_B_3_7),
        "session": spread(itok_B_0_7),
        "chan_len": spread(_lenS),
        "time_len": spread(itok_B_2182_4065),
        "ident": np.eye(P, dtype=np.float32),
        "expand": (p[:, None] // NA == p[None, :] % R).astype(np.float32),
        "rows": np.stack([p, p % NA], axis=1).astype(np.float32),
    }
    arrays = {name: np.ascontiguousarray(a) for name, a in arrays.items()}
    nc = bacc.Bacc("TRN2", target_bir_lowering=False, num_devices=1)
    args = {name: nc.dram_tensor(name, a.shape, mybir.dt.from_np(a.dtype), kind="ExternalInput").ap()
            for name, a in arrays.items()}
    out = nc.dram_tensor("out", [NG * D, GT], F32, kind="ExternalOutput").ap()
    build(nc, **args, out=out)
    result = run_bass_kernel_spmd(nc, [arrays], core_ids=[0]).results[0]["out"]
    return result.reshape(NG, D, GT).transpose(0, 2, 1).reshape(B, C, D)
```

```python
from contextlib import ExitStack

import numpy as np

import concourse.bass as bass
from concourse import mybir

F32 = mybir.dt.float32
F32R = mybir.dt.float32r
BF16 = mybir.dt.bfloat16
F16 = mybir.dt.float16
I32 = mybir.dt.int32
ALU = mybir.AluOpType
ACT = mybir.ActivationFunctionType

P = 128
B, C, D = 32, 128, 2048
NA, R = 8, 16
H, M = 16, 512
NS, HID = 8, 256
NK = D // P
GB = 4
GT = GB * C
NG = B // GB
HQ = 4
NQ = H // HQ
MT = M // P
KG = 7 * R
NIT = NQ * NG
STEPS = NIT * HQ
UNROLL = 8
LAST = STEPS // UNROLL
AHEAD = 2
KC = NK // HQ
CREDIT = 1


def earlier(i, k, lag):
    i2, k2 = i + (k - lag) // UNROLL, (k - lag) % UNROLL
    if isinstance(i, int) and not 0 <= i2 < LAST:
        return None
    return i2, k2


def step_loop(engine, body, tail):
    for k in range(UNROLL):
        body(0, k, k // HQ + AHEAD)
    with engine.Fori(1, (NG - AHEAD) // 2) as i:
        for k in range(UNROLL):
            body(i, k, 2 * i + (k // HQ + AHEAD))
    with engine.Fori((NG - AHEAD) // 2, LAST) as i:
        for k in range(UNROLL):
            body(i, k, None)
    for k in range(tail):
        body(LAST, k, None)


def stage0_order(chunk, select, weights):
    pairs = {2: (0, 1), 3: (2,), 4: (3, 4), 5: (5, 6), 6: (7,)}
    for n in range(AHEAD * HQ):
        chunk(n // HQ, n % HQ)
        for pair in pairs.get(n, ()):
            weights(pair)
        if n % HQ == HQ - 1:
            select(n // HQ)


def wait(engine, sem, count):
    if not (isinstance(count, int) and count <= 0):
        engine.wait_ge(sem, count)


def build(nc, xT, adown, bdown, up, down, w_sess, b_sess, w2, b2, qw, dense, perm, perm_row,
          adapter, session, chan_len, time_len, ident, expand, rows, out):
    with ExitStack() as top:
        def sem(name):
            return top.enter_context(nc.semaphore(name))

        def sb(ctx, name, shape, dt):
            return ctx.enter_context(nc.sbuf_tensor(name, shape, dt))

        g_dram = nc.dram_tensor("g_parts", [H, 3, R, NA, M], BF16).ap()
        bx_dram = nc.dram_tensor("bx_parts", [NG, P, GT], BF16).ap()
        ws_dram = nc.dram_tensor("ws_parts", [NS * C + 1, 2 * HID], F32).ap()
        y_dram = nc.dram_tensor("y_rows", [NIT, P, HQ, GT], F32).ap()
        x1_dram = nc.dram_tensor("x1_rows", [NG * D, GT], F32).ap()

        ident_sb = sb(top, "ident_sb", [P, P], F32)
        rows_sb = sb(top, "rows_sb", [P, 2], F32)
        perm_sb = sb(top, "perm_sb", [P, NK], I32)
        shift = sb(top, "shift", [P, NK], I32)
        ysum = sb(top, "ysum", [P, STEPS], F32)
        dense_sb = sb(top, "dense_sb", [P, 3, NK], F32)
        nzero = sb(top, "nzero", [P, NK], F32)
        ones = sb(top, "ones", [P, P], F32)
        ytot = sb(top, "ytot", [P, B], F32)

        st01 = ExitStack()
        x_idx = sb(st01, "x_idx", [P, NIT, HQ], I32)
        w_idx = sb(st01, "w_idx", [P, NIT, GB], I32)
        ad_v = sb(st01, "ad_v", [P, NIT + 1, GB], I32)
        time_f = sb(st01, "time_f", [P, B], F32)
        permrow_f = sb(st01, "permrow_f", [P, D], F16)
        bias_v = sb(st01, "bias_v", [P, 2, B], F32)
        b2_sb = sb(st01, "b2_sb", [P, 1], F32)
        w2h = sb(st01, "w2h", [P, 2, P], F32R)
        w2l = sb(st01, "w2l", [P, 2, P], F32R)
        gw = sb(st01, "gw", [P, HQ, NA, M], BF16)
        bxw = sb(st01, "bxw", [P, 2, GT], BF16)
        xt = sb(st01, "xt", [P, 2, HQ, GT], F32)

        psum = top.enter_context(nc.psum_tensor("psum", [P, 8, 512], F32))

        s_small = sem("small_loaded")
        s_tab = sem("tables_ready")
        s_perm = sem("perm_loaded")
        s_up = [sem(f"up_loaded{n}") for n in range(2)]
        s_bld = sem("b_loaded")
        s_apg = sem("a_rows_loaded")
        s_acol = sem("a_tiles_picked")
        s_xc = [sem(f"x_chunk_loaded{c}") for c in range(2)]
        s_xcu = sem("x_chunk_used")
        s_draw = sem("down_loaded")
        s_dpart = sem("down_part_made")
        s_gmm = sem("g_product")
        s_ghi = sem("g_high")
        s_gmid = sem("g_middle")
        s_gsp = sem("g_split")
        s_gst = [sem(f"g_stored{n}") for n in range(2)]
        s_bxa = sem("bx_chunk_added")
        s_bxe = sem("bx_copied")
        s_sel = sem("select_ready")
        s_bxs = sem("bx_selected")
        s_bsp = sem("bx_split")
        s_bst = sem("bx_stored")
        s_bst1 = sem("later_bx_stored")
        s_wsp = sem("w_split")
        s_wst = sem("w_stored")
        s_dhi = sem("down_high")
        s_dv = sem("vector_step")
        s_bmid = sem("bx_middle")
        s_tot = sem("y_totals")
        s_ph1 = sem("stage0_done")

        st0 = ExitStack()
        up_sb = sb(st0, "up_sb", [P, 2, 2, M], F32)
        arow = sb(st0, "arow", [P, NK, P], F32)
        acol = sb(st0, "acol", [P, 2, 2, P], F32)
        zrow = sb(st0, "zrow", [1, 2 * HID], F32)
        gpart = sb(st0, "gpart", [P, 2, 3, 2, M], BF16)
        grest = sb(st0, "grest", [P, 2, M], F32)
        cmask = sb(st0, "cmask", [P, B], F32)
        w_row = sb(st0, "w_row", [P, 2, B], F32)
        wraw = sb(st0, "wraw", [P, NS, HID], F32)
        wsp = sb(st0, "wsp", [P, NS, 2, HID], F32R)
        draw0 = sb(st0, "draw0", [P, HQ, MT * P], F32)
        w2raw = sb(st0, "w2raw", [P, 2, P], F32)
        ad_i = sb(st0, "ad_i", [P, B], I32)
        se_i = sb(st0, "se_i", [P, B], I32)
        cl_i = sb(st0, "cl_i", [P, B], I32)
        tl_i = sb(st0, "tl_i", [P, B], I32)
        pr_i = sb(st0, "pr_i", [P, D], I32)
        bs_sb = sb(st0, "bs_sb", [P, 2, NS], F32)
        seq = sb(st0, "seq", [P, NS, B], F32)
        pmod = sb(st0, "pmod", [P, NK], I32)
        st0.close()

        st1 = ExitStack()
        xch_ = sb(st1, "x1c_h", [P, 2, GB, HQ * P], F32R)
        xcl_ = sb(st1, "x1c_l", [P, 2, GB, HQ * P], F32R)
        ws = sb(st1, "ws", [P, 2, GB, 2, HID], F32R)
        raw = sb(st1, "act_raw", [P, 3, 2, 512], F32)
        ah = sb(st1, "act_h", [P, 2, 2, 2, 512], F32R)
        al = sb(st1, "act_l", [P, 2, 2, 2, 512], F32R)
        mh = sb(st1, "mixer_h", [P, 2, 512], F32R)
        ml = sb(st1, "mixer_l", [P, 2, 512], F32R)
        yb = sb(st1, "y_biased", [P, 512], F32)
        ym = sb(st1, "y_masked", [P, 512], F32)
        yt = sb(st1, "y_turned", [P, HQ, P], F32)
        sx_idx = sb(st1, "step_x_idx", [P, 2, HQ], I32)
        sw_idx = sb(st1, "step_w_idx", [P, 2, GB], I32)
        std = ExitStack()
        dwt = sb(std, "dwt", [P, HQ, 2, MT, P], F32R)
        stb = ExitStack()
        bcol = sb(stb, "bcol", [P, NK, P], F32)
        xch = sb(stb, "xch", [P, 2, KC // 2, GT], F32)
        bx_sb = sb(stb, "bx_sb", [P, GT], F32)
        bxp = sb(stb, "bxp", [P, 3, GT], BF16)
        sel = sb(stb, "sel", [P, GB, P], F32)
        expand_sb = sb(stb, "expand_sb", [P, P], F32)
        amask = sb(stb, "amask", [P, B], F32)
        stb.close()
        stc = ExitStack()
        draw = sb(stc, "draw", [P, HQ, MT * P], F32)
        stc.close()
        stq = ExitStack()
        qraw = [sb(stq, f"qraw{n}", [P, D], I32) for n in range(2)]
        stq.close()
        std.close()
        sb(stq, "under_qraw2", [P, (2 * HQ * MT * P - D)], F32)
        qraw.append(sb(stq, "qraw2", [P, D], I32))
        stq.close()
        st1.close()
        st01.close()

        U = [psum[:, 0:2, :], psum[:, 2:4, :]]
        DN, TX, YP, TY = (psum[:, b, :] for b in range(4, 8))

        s_gld = [sem(f"g_loaded{n}") for n in range(HQ)]
        s_bld1 = [sem(f"bx_loaded{n}") for n in range(2)]
        s_wld = [sem(f"w_loaded{n}") for n in range(2)]
        s_dld = sem("down_parts_ready")
        s_xld = [sem(f"x_rows_loaded{n}") for n in range(2)]
        s_x1st = [sem(f"x1_rows_stored{n}") for n in range(2)]
        s_seen = sem("pool_waited")
        s_sp_seen = sem("sync_waited")
        s_idx = sem("step_idx_ready")
        s_u = sem("hidden_product")
        s_gl = sem("gelu_done")
        s_gs = sem("gelu_split")
        s_dn = sem("down_product")
        s_x1 = sem("x1_ready")
        s_tx = sem("x1_turned")
        s_xh = sem("x1c_high")
        s_xl = sem("x1c_split")
        s_m1 = sem("mixer_product")
        s_gl1 = sem("mixer_gelu")
        s_gh1 = sem("mixer_high")
        s_gs1 = sem("mixer_split")
        s_m2 = sem("y_product")
        s_yb = sem("y_bias_added")
        s_ym = sem("y_mask_applied")
        s_ty = sem("y_turned_product")
        s_ye = sem("y_turned_copied")
        s_yst = sem("y_stored")
        s_ytail = [sem(f"y_tail_stored{n}") for n in range(2)]

        st2 = ExitStack()
        q_sb = sb(st2, "q_sb", [P, NK, D], F32R)
        sum_sb = sb(st2, "sum_sb", [P, NG, GT], F32)
        yr = sb(st2, "yr", [P, 4, GT], F32)
        yh = sb(st2, "yh", [P, 4, GT], F32R)
        yl = sb(st2, "yl", [P, 4, GT], F32R)
        sdiag = sb(st2, "sdiag", [P, 2, GB, P], F32)
        dt_ = sb(st2, "dense_t", [P, 8, GT], F32)
        x1r = sb(st2, "x1r", [P, 4, GT], F32)
        st2.close()

        s_ph2 = sem("stage1_done")
        s_q = [sem(f"q_rows_loaded{n}") for n in range(3)]
        s_qb = sem("q_bits")
        s_qf = sem("q_ready")
        s_sd = sem("sum_diag")
        s_sm = sem("sum_product")
        s_se = sem("sum_copied")
        s_yld = [sem(f"y_loaded{n}") for n in range(4)]
        s_yh = sem("y_high")
        s_ysp = sem("y_split")
        s_yu = sem("y_used")
        s_x1l = [sem(f"x1_loaded{n}") for n in range(4)]
        s_acc = sem("dense_product")
        s_t = sem("zero_point_applied")
        s_du = sem("scale_applied")
        s_o = sem("out_ready")
        s_os = [sem(f"out_stored{n}") for n in range(8)]

        block = top.enter_context(nc.Block())
        SMALL = 16 * 13

        def wait_y_used(eng, g, half, k):
            hh = 2 * g + half
            if k >= 4:
                wait(eng, s_yu, hh * (NK - 1) + k - 3)
            elif not (isinstance(hh, int) and hh == 0):
                if k < 3:
                    eng.wait_ge(s_yu, (hh - 1) * (NK - 1) + k + NK - 3)
                else:
                    eng.wait_ge(s_acc, hh * 8)

        def store_first_bx(eng, g):
            for lo, part in ((0, 0), (32, 1), (64, 2), (96, 0)):
                eng.dma_start(bx_dram[g, lo:lo + 32, :], bxp[lo:lo + 32, part, :]).then_inc(s_bst, 16)

        def wait_stage1_stores(eng):
            eng.wait_ge(s_yst, 16 * (STEPS - UNROLL) + CREDIT)
            for n in range(2):
                eng.wait_ge(s_ytail[n], 16 * UNROLL // 2)
            for par in range(2):
                eng.wait_ge(s_x1st[par], 16 * HQ * NIT // 2)

        def enter_stage1(eng):
            eng.wait_ge(s_ph1, 4)

        @block.sync
        def _(sp):
            sp.dma_start(perm_sb[:], perm[:]).then_inc(s_perm, 16)
            sp.dma_start(bcol[:], bdown.rearrange("(k p) r -> p k r", p=P)).then_inc(s_bld, 16)

            def load_chunk(g, c):
                for h in range(2):
                    row = g * D + (c * KC + h * (KC // 2)) * P
                    row = row if isinstance(row, int) else sp.snap(row)
                    wait(sp, s_xcu, 2 * (HQ * g + c) + h - 1)
                    sp.dma_start(xch[:, h, :, :],
                                 xT[bass.ds(row, KC // 2 * P), :].rearrange("(k p) t -> p k t", p=P)).then_inc(s_xc[h], 16)

            def load_up(n):
                wait(sp, s_gmm, n - 1)
                sp.dma_start(up_sb[:, n % 2, :, :].rearrange("p h m -> p (h m)"),
                             up[:, n * 2 * M:(n + 1) * 2 * M]).then_inc(s_up[n % 2], 16)

            def load_down(q, dst):
                sp.dma_start(dst[:].rearrange("p a m -> p (a m)"),
                             down[:, q * HQ * MT * P:(q + 1) * HQ * MT * P]).then_inc(s_draw, 16)

            for n in range(AHEAD * HQ):
                load_chunk(n // HQ, n % HQ)
                if n == 1:
                    load_down(0, draw0)
                    load_up(0)
                    load_up(1)
                elif 2 <= n:
                    load_up(n)

            def load_bx(g, par, free, stored):
                g = g if isinstance(g, int) else sp.snap(g)
                if not (isinstance(stored, int) and stored == 0):
                    wait(sp, s_bst1, stored)
                    sp.sem_inc(s_sp_seen, 1)
                wait(sp, s_u, free)
                sp.dma_start(bxw[:, par, :],
                             bx_dram[bass.ds(g, 1), :, :].rearrange("o p m -> (o p) m")).then_inc(s_bld1[par], 16)

            for q in range(NQ):
                for hq in range(HQ):
                    h = q * HQ + hq
                    wait(sp, s_u, 2 * (STEPS // NQ * q - HQ + 1 + hq) if q else 0)
                    if h % 2 == 0:
                        sp.wait_ge(s_gst[h // 2 % 2], 48 * (h // 4 + 1))
                    for rep in range(4):
                        parts, lo, n = ((0, 2), 2 * R * rep, 2 * R) if rep < 3 else ((2, 3), 6 * R, R)
                        sp.dma_start(gw[lo:lo + n, hq, :, :].rearrange("p a m -> p (a m)"),
                                     g_dram[h, parts[0]:parts[1], :, :, :].rearrange("x r a m -> (x r) (a m)")).then_inc(s_gld[hq], 16)

                def iteration(j, par):
                    it = NG * q + 2 * j + par
                    ahead = q == 0 and not (isinstance(j, int) and j == NG // 2 - 1)
                    if ahead:
                        for c in range(1 if isinstance(it, int) and it == 0 else 0, HQ):
                            load_chunk(it + AHEAD, c)
                    if not (isinstance(j, int) and it == NIT - 1):
                        last = isinstance(j, int) and j == NG // 2 - 1 and par == 1
                        load_bx((2 * j + par + 1) % NG, 1 - par, 2 * HQ * it, 0 if q or last else 64 * it)
                if q == 0:
                    load_chunk(AHEAD, 0)
                    sp.wait_ge(s_bst, 64)
                    load_bx(0, 0, 0, 0)
                    sp.wait_ge(s_bsp, AHEAD)
                    store_first_bx(sp, AHEAD - 1)
                    sp.wait_ge(s_bst, 64 * AHEAD)
                iteration(0, 0)
                iteration(0, 1)
                with sp.Fori(1, NG // 2 - 1) as j:
                    iteration(j, 0)
                    iteration(j, 1)
                if q + 1 < NQ:
                    if q == 0:
                        sp.wait_ge(s_bst1, 64 * (NG - AHEAD))
                    else:
                        sp.wait_ge(s_dld, HQ * (q + 1))
                    load_down(q + 1, draw)
                iteration(NG // 2 - 1, 0)
                iteration(NG // 2 - 1, 1)

            sp.wait_ge(s_ph2, 4)
            wait_stage1_stores(sp)

            def load_half(g, half):
                for k in range(NK):
                    n = k % 4
                    it = g + NG * (k // HQ)
                    it = it if isinstance(it, int) else sp.snap(it)
                    wait(sp, s_ysp, (2 * g + half) * NK + k - 3)
                    sp.dma_start(yr[:, n, :],
                                 y_dram[bass.ds(it, 1), :, k % HQ, :].rearrange("o p t -> (o p) t")).then_inc(s_yld[n], 16)
                    if 6 <= k < 14 and not (isinstance(g, int) and g == 0 and half == 0):
                        load_x1(g, half, k - 6)

            def load_x1(g, half, n):
                row = g * D + (half - 1) * 8 * P + n * P
                row = row if isinstance(row, int) else sp.snap(row)
                if n == 0 and isinstance(g, int):
                    sp.wait_ge(s_qf, NK)
                wait(sp, s_o, (2 * g + half - 1) * 8 + n - 3)
                sp.dma_start(x1r[:, n % 4, :], x1_dram[bass.ds(row, P), :]).then_inc(s_x1l[n % 4], 16)

            load_half(0, 0)
            load_half(0, 1)
            with sp.Fori(1, NG) as g:
                load_half(g, 0)
                load_half(g, 1)
            for n in range(8):
                load_x1(NG, 0, n)
            for n in range(8):
                sp.wait_ge(s_os[n], 16 * NG * 2)

        @block.gpsimd
        def _(pool):
            pool.wait_ge(s_perm, 16)
            for k in range(NK):
                nc.gpsimd.indirect_dma_start(
                    arow[:, k, :], None, adown[:],
                    bass.IndirectOffsetOnAxis(ap=perm_sb[:, k:k + 1], axis=0)).then_inc(s_apg, 16)
            pool.wait_ge(s_apg, 16 * NK)
            pool.wait_ge(s_tab, 1)

            def gather_x(it, par, n):
                nc.gpsimd.tensor_copy(sx_idx[:, par, :], x_idx[:, bass.ds(it, 1), :].rearrange("p o h -> p (o h)")).then_inc(s_idx, 1)
                pool.wait_ge(s_idx, n)
                pool.sem_inc(s_seen, 1)
                for hq in range(HQ):
                    nc.gpsimd.indirect_dma_start(
                        xt[:, par, hq, :], None, xT[:],
                        bass.IndirectOffsetOnAxis(ap=sx_idx[:, par, hq:hq + 1], axis=0)).then_inc(s_xld[par], 16)

            def gather_w(it, par, n):
                nc.gpsimd.tensor_copy(sw_idx[:, par, :], w_idx[:, bass.ds(it, 1), :].rearrange("p o h -> p (o h)")).then_inc(s_idx, 1)
                pool.wait_ge(s_idx, n)
                pool.sem_inc(s_seen, 1)
                for b in range(GB):
                    nc.gpsimd.indirect_dma_start(
                        ws[:, par, b, :, :].rearrange("p x h -> p (x h)").bitcast(F32), None, ws_dram[:],
                        bass.IndirectOffsetOnAxis(ap=sw_idx[:, par, b:b + 1], axis=0)).then_inc(s_wld[par], 16)

            def scatter_x1(it, par, hq):
                pool.wait_ge(s_x1, HQ * it + hq + 1)
                pool.sem_inc(s_seen, 1)
                nc.gpsimd.indirect_dma_start(
                    x1_dram[:], bass.IndirectOffsetOnAxis(ap=sx_idx[:, par, hq:hq + 1], axis=0),
                    xt[:, par, hq, :], None).then_inc(s_x1st[par], 16)

            pool.sem_inc(s_ph1, 1)
            gather_x(0, 0, 1)
            gather_x(1, 1, 2)
            enter_stage1(pool)
            pool.wait_ge(s_wst, 32)
            gather_w(0, 0, 3)

            def down_parts(q, hq):
                pool.wait_ge(s_draw, 16 * (q + 1))
                nc.gpsimd.tensor_copy(dwt[:, hq, 0, :, :].rearrange("p m d -> p (m d)"), draw[:, hq, :]).then_inc(s_dpart, 1)
                pool.wait_ge(s_dpart, (q - 1) * HQ + hq + 1)
                nc.gpsimd.tensor_tensor(dwt[:, hq, 1, :, :].rearrange("p m d -> p (m d)"), draw[:, hq, :],
                                        dwt[:, hq, 0, :, :].rearrange("p m d -> p (m d)").bitcast(F32),
                                        ALU.subtract).then_inc(s_dld, 1)

            def later_bx(g):
                if isinstance(g, int) and g == AHEAD:
                    pool.wait_ge(s_bst, 64 * AHEAD)
                else:
                    pool.wait_ge(s_bst1, 64 * (g - AHEAD))
                    pool.sem_inc(s_seen, 1)
                pool.wait_ge(s_bxe, g + 1)
                pool.sem_inc(s_seen, 1)
                nc.gpsimd.tensor_copy(bxp[:, 0, :], bx_sb[:]).then_inc(s_bmid, 1)
                pool.wait_ge(s_bmid, 3 * g + 1)
                pool.sem_inc(s_seen, 1)
                nc.gpsimd.tensor_tensor(bx_sb[:], bx_sb[:], bxp[:, 0, :], ALU.subtract).then_inc(s_bmid, 1)
                pool.wait_ge(s_bmid, 3 * g + 2)
                pool.sem_inc(s_seen, 1)
                nc.gpsimd.tensor_copy(bxp[:, 1, :], bx_sb[:]).then_inc(s_bmid, 1)
                pool.wait_ge(s_bmid, 3 * g + 3)
                pool.sem_inc(s_seen, 1)
                nc.gpsimd.tensor_tensor(bxp[:, 2, :], bx_sb[:], bxp[:, 1, :], ALU.subtract).then_inc(s_bsp, 1)
                pool.wait_ge(s_bsp, g + 1)
                pool.sem_inc(s_seen, 1)
                for lo, part in ((0, 0), (32, 1), (64, 2), (96, 0)):
                    pool.dma_start(bx_dram[bass.ds(g, 1), lo:lo + 32, :].rearrange("o p t -> (o p) t"),
                                   bxp[lo:lo + 32, part, :]).then_inc(s_bst1, 16)

            def iteration(it, par, quad, group):
                for hq in range(HQ):
                    if hq == HQ - 1 and group is not None:
                        later_bx(group)
                    scatter_x1(it, par, hq)
                    if quad is not None and quad + 1 < NQ:
                        down_parts(quad + 1, hq)
                if not (isinstance(it, int) and it >= NIT - 2):
                    pool.wait_ge(s_tx, HQ * (it + 1))
                    pool.wait_ge(s_x1st[par], 16 * HQ * ((it - par) // 2 + 1))
                    pool.sem_inc(s_seen, 1)
                    gather_x(it + 2, par, 2 * it + 4)
                if not (isinstance(it, int) and it == NIT - 1):
                    wait(pool, s_m1, HQ * it)
                    pool.sem_inc(s_seen, 1)
                    gather_w(it + 1, 1 - par, 2 * it + 5 if not (isinstance(it, int) and it >= NIT - 2) else 2 * NIT)

            def gather_q(k):
                nc.gpsimd.indirect_dma_start(
                    qraw[k % 3][:], None, qw[:],
                    bass.IndirectOffsetOnAxis(ap=perm_sb[:, k:k + 1], axis=0)).then_inc(s_q[k % 3], 16)

            for q in range(NQ):
                def pair(j):
                    for par in range(2):
                        it = NG * q + 2 * j + par
                        final = isinstance(j, int) and j == NG // 2 - 1
                        iteration(it, par, q if final and par == 1 else None,
                                  it + AHEAD if q == 0 and not final else None)

                pair(0)
                with pool.Fori(1, NG // 2 - 1) as j:
                    pair(j)
                if q == NQ - 1:
                    pool.wait_ge(s_dld, H)
                    gather_q(0)
                    gather_q(1)
                pair(NG // 2 - 1)
            gather_q(2)
            pool.sem_inc(s_ph2, 1)
            pool.wait_ge(s_ph2, 4)
            for k in range(3, NK):
                pool.wait_ge(s_qf, k - 2)
                gather_q(k)
            with pool.Fori(0, 2 * NG) as hh:
                for n in range(8):
                    row = pool.snap(hh * 8 * P + n * P)
                    pool.wait_ge(s_o, hh * 8 + n + 1)
                    pool.sem_inc(s_seen, 1)
                    pool.dma_start(out[bass.ds(row, P), :], dt_[:, n, :]).then_inc(s_os[n], 16)

        @block.tensor
        def _(pe):
            pe.wait_ge(s_bld, 16)

            def weights(g):
                par = g % 2
                pe.wait_ge(s_up[par], 16 * (g // 2 + 1))
                pe.wait_ge(s_acol, g + 1)
                wait(pe, s_gsp, g - 1)
                for n in range(2):
                    mm = nc.tensor.matmul(psum[:, 2 * par + n, :], acol[:, par, n, :], up_sb[:, par, n, :],
                                          start=True, stop=True)
                mm.then_inc(s_gmm, 1)

            def bx_chunk(g, c):
                n = HQ * g + c
                wait(pe, s_bxa, n)
                for k in range(KC):
                    h = k // (KC // 2)
                    if k % (KC // 2) == 0:
                        pe.wait_ge(s_xc[h], 16 * (n + 1))
                    mm = nc.tensor.matmul(TY, bcol[:, c * KC + k, :], xch[:, h, k % (KC // 2), :],
                                          start=(k == 0), stop=(k == KC - 1))
                    if k % (KC // 2) == KC // 2 - 1:
                        mm.then_inc(s_xcu, 1)

            def bx_select(g):
                pe.wait_ge(s_bxa, HQ * (g + 1))
                pe.wait_ge(s_sel, g + 1)
                if isinstance(g, int) and g < AHEAD:
                    wait(pe, s_bxe, g)
                for b in range(GB):
                    mm = nc.tensor.matmul(YP[:, b * C:(b + 1) * C], sel[:, b, :],
                                          bx_sb[:, b * C:(b + 1) * C], start=True, stop=True)
                mm.then_inc(s_bxs, 1)

            stage0_order(bx_chunk, bx_select, weights)
            pe.wait_ge(s_bxe, AHEAD)
            pe.wait_ge(s_gsp, H // 2)
            pe.sem_inc(s_ph1, 1)
            pe.wait_ge(s_tab, 1)

            adapters = ad_v[0:1, :, :].rearrange("p i b -> p (i b)")
            regs = [[pe.alloc_register(f"adapter{par}_{b}") for b in range(GB)] for par in range(2)]
            chosen = [None] * GB

            def load_adapters(it, par):
                for b in range(GB):
                    pe.reg_load(regs[par][b], adapters[:, bass.ds(it * GB + b, 1)])

            def hidden(i, k, part):
                u = U[(k + part) % 2]
                for m in range(2):
                    for b in range(GB):
                        col = (2 * part + m) * P
                        g_tile = gw[0:KG, k % HQ, bass.ds(chosen[b], 1), col:col + P].rearrange("p o m -> p (o m)")
                        mm = nc.tensor.matmul(u[:, m, b * C:(b + 1) * C], g_tile,
                                              bxw[0:KG, k // HQ, b * C:(b + 1) * C], start=True, stop=True)
                mm.then_inc(s_u, 1)

            def step(i, k, group):
                s = UNROLL * i + k
                now, dn, tx = earlier(i, k, 0), earlier(i, k, 1), earlier(i, k, 2)
                m1, m2, ty = earlier(i, k, 6), earlier(i, k, 7), earlier(i, k, 8)

                def down_half(half):
                    j = UNROLL * dn[0] + dn[1]
                    par, hq = dn[1] // HQ, dn[1] % HQ
                    if half == 0:
                        if par == 0:
                            pe.wait_ge(s_dld, dn[0] // (NG // 2) * HQ + (hq + 1))
                        pe.wait_ge(s_gs, 2 * j + 2)
                        if not tx:
                            wait(pe, s_x1, j)
                    for m in range(half * MT // 2, (half + 1) * MT // 2):
                        for n, (w, a) in enumerate(((0, ah), (1, ah), (0, al))):
                            mm = nc.tensor.matmul(DN, dwt[:, hq, w, m, :], a[:, dn[1] % 2, m // 2, m % 2, :],
                                                  start=(m == 0 and n == 0), stop=(m == MT - 1 and n == 2))
                    if half == 1:
                        mm.then_inc(s_dn, 1)

                def turn_y():
                    v = UNROLL * ty[0] + ty[1]
                    pe.wait_ge(s_ym, v + 1)
                    if group is None:
                        wait(pe, s_ye, v + CREDIT)
                    else:
                        pe.wait_ge(s_bxa, HQ * group + k % HQ + 1)
                    for t in range(HQ):
                        mm = nc.tensor.transpose(TY[:, t * P:(t + 1) * P], ym[:, t * P:(t + 1) * P], ident_sb[:])
                    mm.then_inc(s_ty, 1)

                def mixer_hidden():
                    v = UNROLL * m1[0] + m1[1]
                    par, b = m1[1] // GB, m1[1] % GB
                    if b == 0:
                        pe.wait_ge(s_wld[par], 16 * GB * (m1[0] + 1))
                        pe.wait_ge(s_xl, v + GB)
                    if now:
                        pe.wait_ge(s_gl, 2 * s + 1)
                    else:
                        pe.wait_ge(s_gl, 2 * STEPS)
                        pe.wait_ge(s_gl1, v - 1)
                    u = U[k % 2]
                    for x in range(2):
                        n = 0
                        for w, a in ((0, xch_), (1, xch_), (0, xcl_)):
                            mm = nc.tensor.matmul(u[:, x, :], ws[:, par, b, w, x * P:(x + 1) * P],
                                                  a[:, par, b, :], start=(n == 0), stop=(n == 2))
                            n += 1
                    mm.then_inc(s_m1, 1)

                def mixer_out():
                    v = UNROLL * m2[0] + m2[1]
                    pe.wait_ge(s_gs1, v + 1)
                    if not (ty and now):
                        wait(pe, s_yb, v)
                    if group is not None and k % HQ == HQ - 1:
                        pe.wait_ge(s_bxe, group + 1)
                    n = 0
                    for x in range(2):
                        for w, a in ((w2h, mh), (w2l, mh), (w2h, ml)):
                            mm = nc.tensor.matmul(YP, w[:, x, :], a[:, x, :],
                                                  start=(n == 0), stop=(n == 5))
                            n += 1
                    mm.then_inc(s_m2, 1)

                if now:
                    if k % HQ == 0:
                        for b in range(GB):
                            chosen[b] = pe.snap(regs[k // HQ][b], min_val=0, max_val=NA - 1)
                        pe.wait_ge(s_bld1[k // HQ], 16 * (i + 1))
                    if k < HQ:
                        pe.wait_ge(s_gld[k], 64 * (i // (NG // 2) + 1))
                    wait(pe, s_gl, 2 * s)
                    hidden(i, k, 0)
                if tx:
                    j = UNROLL * tx[0] + tx[1]
                    pe.wait_ge(s_x1, j + 1)
                    wait(pe, s_xl, j)
                    for b in range(GB):
                        mm = nc.tensor.transpose(TX[:, b * C:(b + 1) * C],
                                                 xt[:, tx[1] // HQ, tx[1] % HQ, b * C:(b + 1) * C], ident_sb[:])
                    mm.then_inc(s_tx, 1)
                if dn:
                    down_half(0)
                if now:
                    if earlier(i, k, 7):
                        pe.wait_ge(s_gl1, s - 6)
                    hidden(i, k, 1)
                if group is not None:
                    if ty:
                        wait(pe, s_ye, UNROLL * ty[0] + ty[1] + CREDIT)
                    bx_chunk(group, k % HQ)
                if dn:
                    down_half(1)
                if now:
                    if ty:
                        turn_y()
                    if group is not None and k % HQ == HQ - 1:
                        bx_select(group)
                    if k % HQ == HQ // 2:
                        load_adapters(2 * i + (k // HQ + 1), 1 - k // HQ)
                    if m1:
                        mixer_hidden()
                    if m2:
                        mixer_out()
                else:
                    if m1:
                        mixer_hidden()
                    if m2:
                        mixer_out()
                    turn_y()

            pe.sem_inc(s_m2, CREDIT)
            load_adapters(0, 0)
            step_loop(pe, step, 8)
            pe.sem_inc(s_ph2, 1)
            pe.wait_ge(s_ph2, 4)

            for g in range(NG):
                pe.wait_ge(s_sd, g + 2)
                nc.tensor.matmul(psum[:, g, :], ones[:], sdiag[:, g % 2, :, :].rearrange("p b t -> p (b t)"),
                                 start=True, stop=True).then_inc(s_sm, 1)

            def dense_group(g):
                for half in range(2):
                    for k in range(NK):
                        pe.wait_ge(s_qf, k + 1)
                        pe.wait_ge(s_ysp, g * 2 * NK + half * NK + k + 1)
                        for n in range(8):
                            if k == 0:
                                if half == 0 and isinstance(g, int):
                                    pe.wait_ge(s_se, n + 1)
                                else:
                                    pe.wait_ge(s_t, g * NK + half * 8 + n - 7)
                            col = (half * 8 + n) * P
                            nc.tensor.matmul(psum[:, n, :], q_sb[:, k, col:col + P], yh[:, k % 4, :],
                                             start=(k == 0), stop=False)
                            mm = nc.tensor.matmul(psum[:, n, :], q_sb[:, k, col:col + P], yl[:, k % 4, :],
                                                  start=False, stop=(k == NK - 1))
                            if k == NK - 1:
                                mm.then_inc(s_acc, 1)
                            elif n == 7:
                                mm.then_inc(s_yu, 1)
            dense_group(0)
            with pe.Fori(1, NG) as g:
                dense_group(g)

        @block.scalar
        def _(act):
            for dst, src in ((ad_i, adapter), (rows_sb, rows), (expand_sb, expand), (se_i, session),
                             (cl_i, chan_len), (tl_i, time_len), (ident_sb, ident), (b2_sb, b2)):
                act.dma_start(dst[:], src[:]).then_inc(s_small, 16)
            act.dma_start(pr_i[:], perm_row[:]).then_inc(s_small, 16)
            act.dma_start(bs_sb[:].rearrange("p a b -> p (a b)"), b_sess[:]).then_inc(s_small, 16)
            act.dma_start(dense_sb[:].rearrange("p a b -> p (a b)"), dense[:]).then_inc(s_small, 16)
            act.dma_start(w2raw[:].rearrange("p a b -> p (a b)"), w2[:]).then_inc(s_small, 16)
            act.dma_start(wraw[:], w_sess[:].rearrange("(s c) h -> c s h", c=C)).then_inc(s_small, 16)

            def prepare(g):
                par = g % 2
                act.wait_ge(s_gmm, g + 1)
                wait(act, s_gst[par], 48 * (g // 2))
                nc.scalar.activation(gpart[:, par, 0, :, :], psum[:, 2 * par:2 * par + 2, :], ACT.Copy).then_inc(s_ghi, 1)
                act.wait_ge(s_gsp, g + 1)
                for part in range(3):
                    act.dma_start(g_dram[2 * g:2 * g + 2, part, :, :, :].rearrange("h r a m -> (r a) h m"),
                                  gpart[:, par, part, :, :]).then_inc(s_gst[par], 16)

            def bx_copy(g):
                act.wait_ge(s_bxs, g + 1)
                nc.scalar.activation(bx_sb[:], YP, ACT.Copy).then_inc(s_bxe, 1)

            def chunk(g, c):
                if (g, c) == (0, 1):
                    act.wait_ge(s_draw, 16)
                    nc.scalar.activation(dwt[:, :, 0, :, :].rearrange("p h m d -> p h (m d)"), draw0[:],
                                         ACT.Copy).then_inc(s_dhi, 1)
                if (g, c) == (1, 1):
                    act.wait_ge(s_wsp, 1)
                    act.dma_start(ws_dram[0:NS * C, :].rearrange("(s c) h -> c s h", c=C),
                                  wsp[:].rearrange("p s x h -> p s (x h)").bitcast(F32)).then_inc(s_wst, 16)
                    act.dma_start(ws_dram[NS * C:NS * C + 1, :], zrow[:]).then_inc(s_wst, 16)

            def select(g):
                bx_copy(g)
                if g < AHEAD - 1:
                    act.wait_ge(s_bsp, g + 1)
                    store_first_bx(act, g)

            stage0_order(chunk, select, prepare)
            act.wait_ge(s_wst, 32)
            for n in range(2):
                act.wait_ge(s_gst[n], 48 * (H // 4))
            act.sem_inc(s_ph1, 1)
            enter_stage1(act)

            def gelu(i, k, part):
                s = UNROLL * i + k
                wait(act, s_dn, s - 1)
                nc.scalar.activation(ah[:, k % 2, part, :, :], U[(k + part) % 2], ACT.Gelu)
                wait(act, s_gs, 2 * s - 1 + part)
                nc.scalar.activation(raw[:, part, :, :], U[(k + part) % 2], ACT.Gelu).then_inc(s_gl, 1)

            def step(i, k, group):
                s = UNROLL * i + k
                now, tx = earlier(i, k, 0), earlier(i, k, 2)
                m1, m2, ty = earlier(i, k, 6), earlier(i, k, 7), earlier(i, k, 8)

                y_buf, y_sem = (yt[:].rearrange("p a b -> p (a b)"), s_yst) if now else (raw[:, 0, k % 2, :], s_ytail[k % 2])

                def copy_turned():
                    v = UNROLL * ty[0] + ty[1]
                    act.wait_ge(s_ty, v + 1)
                    if now:
                        wait(act, s_yst, 16 * v + CREDIT)
                    else:
                        act.wait_ge(s_gs, 2 * STEPS)
                        wait(act, y_sem, 16 * (k // 2))
                    nc.scalar.activation(y_buf, TY, ACT.Copy).then_inc(s_ye, 1)

                def mixer_gelu():
                    v = UNROLL * m1[0] + m1[1]
                    act.wait_ge(s_m1, v + 1)
                    wait(act, s_gs1, v)
                    b = UNROLL * (m1[0] % (NG // 2)) + m1[1]
                    for x in range(2):
                        a = nc.scalar.activation(raw[:, 2, x, :], U[k % 2][:, x, :], ACT.Gelu,
                                                 bias=bias_v[:, x, bass.ds(b, 1)])
                    a.then_inc(s_gl1, 1)

                def store_turned():
                    act.wait_ge(s_ye, UNROLL * ty[0] + ty[1] + 1 + CREDIT)
                    y_dst = y_dram[bass.ds(2 * ty[0] + ty[1] // GB, 1), :, :, ty[1] % GB * C:(ty[1] % GB + 1) * C]
                    act.dma_start(y_dst.rearrange("o p k t -> (o p) k t"), y_buf.rearrange("p (k t) -> p k t", t=C)).then_inc(y_sem, 16)

                def add_b2():
                    v = UNROLL * m2[0] + m2[1]
                    act.wait_ge(s_m2, v + 1 + CREDIT)
                    wait(act, s_ym, v)
                    nc.scalar.activation(yb[:], YP, ACT.Identity, bias=b2_sb[:, 0:1]).then_inc(s_yb, 1)

                if now:
                    act.wait_ge(s_u, 2 * s + 1)
                    gelu(i, k, 0)
                if tx:
                    j = UNROLL * tx[0] + tx[1]
                    act.wait_ge(s_tx, j + 1)
                    if tx[1] % HQ == 0:
                        wait(act, s_m1, j - HQ)
                    dst = xch_[:, tx[1] // HQ, :, tx[1] % HQ * P:(tx[1] % HQ + 1) * P]
                    nc.scalar.activation(dst, TX.rearrange("p (b t) -> p b t", b=GB), ACT.Copy).then_inc(s_xh, 1)
                if now:
                    act.wait_ge(s_u, 2 * s + 2)
                    gelu(i, k, 1)
                if now:
                    if ty:
                        copy_turned()
                    if group is not None and k % HQ == HQ - 1:
                        bx_copy(group)
                    if m1:
                        mixer_gelu()
                    if ty:
                        store_turned()
                    if m2:
                        add_b2()
                else:
                    if m1:
                        mixer_gelu()
                    if m2:
                        add_b2()
                    copy_turned()
                    store_turned()

            act.sem_inc(s_ye, CREDIT)
            act.sem_inc(s_yst, CREDIT)
            step_loop(act, step, 8)
            act.wait_ge(s_ye, STEPS + CREDIT)
            act.sem_inc(s_ph2, 1)
            act.wait_ge(s_ph2, 4)
            wait_stage1_stores(act)

            def unpack(k):
                act.wait_ge(s_qb, k + 1)
                nc.scalar.activation(q_sb[:, k, :], qraw[k % 3][:], ACT.Copy).then_inc(s_qf, 1)

            def y_high(g, half, k):
                act.wait_ge(s_yld[k % 4], 16 * (8 * g + 4 * half + k // 4 + 1))
                wait_y_used(act, g, half, k)
                nc.scalar.activation(yh[:, k % 4, :], yr[:, k % 4, :], ACT.Copy).then_inc(s_yh, 1)

            def scale(g, half):
                for n in range(8):
                    nn = 8 * (1 - half) + n
                    act.wait_ge(s_t, (2 * g + half - 1) * 8 + n + 1)
                    nc.scalar.activation(dt_[:, n, :], dt_[:, n, :], ACT.Identity, bias=dense_sb[:, 2, nn:nn + 1],
                                         scale=dense_sb[:, 0, nn:nn + 1]).then_inc(s_du, 1)

            def half_group(g, half):
                for k in range(3):
                    y_high(g, half, k)
                scale(g, half)
                for k in range(3, NK):
                    y_high(g, half, k)

            unpack(0)
            unpack(1)
            for bank in range(NG):
                act.wait_ge(s_sm, bank + 1)
                nc.scalar.activation(sum_sb[:, bank, :], psum[:, bank, :], ACT.Copy).then_inc(s_se, 1)
            for k in range(NK):
                if 2 <= k + 1 < NK:
                    unpack(k + 1)
                y_high(0, 0, k)
            half_group(0, 1)
            with act.Fori(1, NG) as g:
                half_group(g, 0)
                half_group(g, 1)
            scale(NG, 0)

        @block.vector
        def _(dve):
            done = 0

            def own(instruction):
                nonlocal done
                done += 1
                instruction.then_inc(s_dv, 1)

            def after_own():
                dve.wait_ge(s_dv, done)

            v = nc.vector

            def tables():
                dve.wait_ge(s_small, SMALL)
                dve.wait_ge(s_perm, 16)
                for g in range(NG):
                    own(v.tensor_scalar(x_idx[:, :, :].rearrange("p (q g) h -> p q g h", g=NG)[:, :, g, :],
                                        perm_sb[:].rearrange("p (q h) -> p q h", h=HQ), g * D, None, ALU.add))
                for q in range(NQ):
                    own(v.tensor_copy(ad_v[:, q * NG:(q + 1) * NG, :].rearrange("p g b -> p (g b)"), ad_i[:]))
                own(v.tensor_copy(ad_v[:, NIT, :], ad_i[:, 0:GB]))
                own(v.tensor_scalar(w_row[:, 0, :], se_i[:], C, rows_sb[:, 0:1], ALU.mult, ALU.add))
                own(v.tensor_scalar(amask[:], ad_i[:], rows_sb[:, 1:2], None, ALU.is_equal))
                own(v.tensor_scalar(cmask[:], cl_i[:], rows_sb[:, 0:1], None, ALU.is_gt))
                own(v.memset(zrow[:], 0.0))
                own(v.tensor_copy(wsp[:, :, 0, :], wraw[:]))
                own(v.tensor_copy(time_f[:], tl_i[:]))
                own(v.tensor_copy(permrow_f[:], pr_i[:]))
                own(v.tensor_scalar(nzero[:], dense_sb[:, 1, :], -1.0, None, ALU.mult))
                own(v.tensor_scalar(pmod[:], perm_sb[:], 3, None, ALU.bitwise_and))
                own(v.memset(bias_v[:], 0.0))
                for n in range(NS):
                    own(v.tensor_scalar(seq[:, n, :], se_i[:], n, None, ALU.is_equal))
                own(v.tensor_copy(w2h[:], w2raw[:]))
                after_own()
                own(v.tensor_scalar(shift[:], pmod[:], 1, 6, ALU.is_equal, ALU.mult))
                own(v.tensor_tensor(w2l[:], w2raw[:], w2h[:].bitcast(F32), ALU.subtract))
                v.tensor_tensor(wsp[:, :, 1, :], wraw[:], wsp[:, :, 0, :].bitcast(F32), ALU.subtract).then_inc(s_wsp, 1)
                own(v.scalar_tensor_tensor(w_row[:, 1, :], w_row[:, 0, :], float(-NS * C), cmask[:], ALU.add, ALU.mult))
                after_own()
                for q in range(NQ):
                    own(v.tensor_scalar(w_idx[:, q * NG:(q + 1) * NG, :].rearrange("p g b -> p (g b)"),
                                        w_row[:, 1, :], float(NS * C), None, ALU.add))
                for n in range(NS):
                    for x in range(2):
                        own(v.scalar_tensor_tensor(bias_v[:, x, :], seq[:, n, :], bs_sb[:, x, n:n + 1],
                                                   bias_v[:, x, :], ALU.mult, ALU.add))
                    after_own()
                v.tensor_copy(seq[:, 0, :], seq[:, 1, :]).then_inc(s_tab, 1)

                dve.wait_ge(s_tab, 1)

            def prepare(g):
                par = g % 2
                part = gpart[:, par, :, :, :]
                if g == 0:
                    dve.wait_ge(s_apg, 16 * NK)
                wait(dve, s_gmm, g)
                for n in ((0, 1) if g == 0 else (g + 1,) if g + 1 < H // 2 else ()):
                    v.tensor_copy(acol[:, n % 2, :, :], arow[:, 2 * n:2 * n + 2, :]).then_inc(s_acol, 1)
                dve.wait_ge(s_ghi, g + 1)
                v.tensor_tensor(grest[:], psum[:, 2 * par:2 * par + 2, :], part[:, 0, :, :], ALU.subtract).then_inc(s_gmid, 1)
                dve.wait_ge(s_gmid, 2 * g + 1)
                v.tensor_copy(part[:, 1, :, :], grest[:]).then_inc(s_gmid, 1)
                dve.wait_ge(s_gmid, 2 * g + 2)
                v.tensor_tensor(part[:, 2, :, :], grest[:], part[:, 1, :, :], ALU.subtract).then_inc(s_gsp, 1)
                dve.wait_ge(s_gsp, g + 1)

            def bx_add(g, c):
                n = HQ * g + c
                if c == HQ - 1:
                    wait(dve, s_bxs, g)
                    for b in range(GB):
                        a = v.tensor_scalar(sel[:, b, :], expand_sb[:], amask[:, bass.ds(g * GB + b, 1)], None, ALU.mult)
                    a.then_inc(s_sel, 1)
                if c == 0:
                    wait(dve, s_bsp, g)
                    dve.wait_ge(s_xcu, 2 * n + 2)
                    v.tensor_copy(bx_sb[:], TY).then_inc(s_bxa, 1)
                else:
                    dve.wait_ge(s_bxa, n)
                    dve.wait_ge(s_xcu, 2 * n + 2)
                    v.tensor_tensor(bx_sb[:], bx_sb[:], TY, ALU.add).then_inc(s_bxa, 1)

            def bx_parts(g):
                dve.wait_ge(s_bxe, g + 1)
                wait(dve, s_bst, 64 * g)
                v.tensor_copy(bxp[:, 0, :], bx_sb[:]).then_inc(s_bmid, 1)
                dve.wait_ge(s_bmid, 3 * g + 1)
                v.tensor_tensor(bx_sb[:], bx_sb[:], bxp[:, 0, :], ALU.subtract).then_inc(s_bmid, 1)
                dve.wait_ge(s_bmid, 3 * g + 2)
                v.tensor_copy(bxp[:, 1, :], bx_sb[:]).then_inc(s_bmid, 1)
                dve.wait_ge(s_bmid, 3 * g + 3)
                v.tensor_tensor(bxp[:, 2, :], bx_sb[:], bxp[:, 1, :], ALU.subtract).then_inc(s_bsp, 1)

            def chunk(g, c):
                bx_add(g, c)
                if (g, c) == (0, 1):
                    tables()
                if (g, c) == (1, 0):
                    dve.wait_ge(s_dhi, 1)
                    v.tensor_tensor(dwt[:, :, 1, :, :].rearrange("p h m d -> p h (m d)"), draw0[:],
                                    dwt[:, :, 0, :, :].rearrange("p h m d -> p h (m d)").bitcast(F32),
                                    ALU.subtract).then_inc(s_dld, 1)
                    dve.sem_inc(s_dld, HQ - 1)

            def select(g):
                if g == AHEAD - 1:
                    dve.wait_ge(s_wsp, 1)
                    dve.wait_ge(s_dld, HQ)
                    dve.sem_inc(s_ph1, 1)
                bx_parts(g)

            stage0_order(chunk, select, prepare)
            enter_stage1(dve)

            def low(par, slot, done_sem):
                v.tensor_tensor(al[:, par, slot, :, :], raw[:, slot, :, :],
                                ah[:, par, slot, :, :].bitcast(F32), ALU.subtract).then_inc(done_sem, 1)

            def bits(k):
                dve.wait_ge(s_q[k % 3], 16 * (k // 3 + 1))
                v.tensor_scalar(qraw[k % 3][:], qraw[k % 3][:], shift[:, k:k + 1], 63,
                                ALU.logical_shift_right, ALU.bitwise_and).then_inc(s_qb, 1)

            def step(i, k, group):
                s = UNROLL * i + k
                now, dn, tx = earlier(i, k, 0), earlier(i, k, 1), earlier(i, k, 2)
                m2, ym_item = earlier(i, k, 7), earlier(i, k, 8)

                def mask():
                    v3 = UNROLL * ym_item[0] + ym_item[1]
                    dve.wait_ge(s_yb, v3 + 1)
                    wait(dve, s_ty, v3)
                    b = UNROLL * (ym_item[0] % (NG // 2)) + ym_item[1]
                    v.scalar_tensor_tensor(ym[:], permrow_f[:, bass.ds(ym_item[0] // (NG // 2) * HQ * P, HQ * P)],
                                           time_f[:, bass.ds(b, 1)], yb[:], ALU.is_lt, ALU.mult,
                                           accum_out=ysum[:, bass.ds(v3, 1)]).then_inc(s_ym, 1)

                def mixer_parts():
                    v2 = UNROLL * m2[0] + m2[1]
                    dve.wait_ge(s_gl1, v2 + 1)
                    wait(dve, s_m2, v2 + CREDIT)
                    v.tensor_copy(mh[:], raw[:, 2, :, :]).then_inc(s_gh1, 1)
                    dve.wait_ge(s_gh1, v2 + 1)
                    v.tensor_tensor(ml[:], raw[:, 2, :, :], mh[:].bitcast(F32), ALU.subtract).then_inc(s_gs1, 1)

                if now:
                    if ym_item:
                        mask()
                    if m2:
                        mixer_parts()
                else:
                    if m2:
                        mixer_parts()
                    mask()
                    if k >= 6:
                        bits(k - 6)
                if now:
                    dve.wait_ge(s_gl, 2 * s + 1)
                    wait(dve, s_dn, s - 1)
                    low(k % 2, 0, s_gs)
                if tx:
                    j = UNROLL * tx[0] + tx[1]
                    dve.wait_ge(s_xh, j + 1)
                    cols = slice(tx[1] % HQ * P, (tx[1] % HQ + 1) * P)
                    par = tx[1] // HQ
                    v.tensor_tensor(xcl_[:, par, :, cols], TX.rearrange("p (b t) -> p b t", b=GB),
                                    xch_[:, par, :, cols].bitcast(F32), ALU.subtract).then_inc(s_xl, 1)
                if now and group is not None:
                    dve.wait_ge(s_gl, 2 * s + 2)
                    low(k % 2, 1, s_gs)
                if group is not None:
                    bx_add(group, k % HQ)
                if dn:
                    j = UNROLL * dn[0] + dn[1]
                    par, hq = dn[1] // HQ, dn[1] % HQ
                    dve.wait_ge(s_dn, j + 1)
                    dve.wait_ge(s_xld[par], 16 * HQ * (dn[0] + 1))
                    v.tensor_tensor(xt[:, par, hq, :], xt[:, par, hq, :], DN, ALU.add).then_inc(s_x1, 1)
                if now and group is None:
                    dve.wait_ge(s_gl, 2 * s + 2)
                    low(k % 2, 1, s_gs)

            step_loop(dve, step, 8)
            for watched, count in ((s_x1, STEPS), (s_ym, STEPS), (s_xl, STEPS), (s_gs1, STEPS)):
                dve.wait_ge(watched, count)
            dve.sem_inc(s_ph2, 1)

            v.memset(ones[:], 1.0).then_inc(s_sd, 1)
            n_tot = 0
            ys = ysum[:].rearrange("p (q b) -> p q b", b=B)
            for a, b in ((ys[:, 0, :], ys[:, 1, :]), (ytot[:], ys[:, 2, :]), (ytot[:], ys[:, 3, :])):
                v.tensor_tensor(ytot[:], a, b, ALU.add).then_inc(s_tot, 1)
                n_tot += 1
                dve.wait_ge(s_tot, n_tot)
            dve.wait_ge(s_ph2, 4)
            for g in range(NG):
                wait(dve, s_sm, g - 1)
                for b in range(GB):
                    a = v.tensor_scalar(sdiag[:, g % 2, b, :], ident_sb[:], ytot[:, g * GB + b:g * GB + b + 1], None, ALU.mult)
                a.then_inc(s_sd, 1)
            bits(2)

            def y_low(g, half, k):
                dve.wait_ge(s_yh, (2 * g + half) * NK + k + 1)
                v.tensor_tensor(yl[:, k % 4, :], yr[:, k % 4, :], yh[:, k % 4, :].bitcast(F32),
                                ALU.subtract).then_inc(s_ysp, 1)

            def zero_point(g, half):
                last_g = g - 1 if half == 0 else g
                for n in range(8):
                    nn = 8 * (1 - half) + n
                    dve.wait_ge(s_acc, (2 * g + half - 1) * 8 + n + 1)
                    wait(dve, s_os[n], 16 * (2 * g + half - 1))
                    v.scalar_tensor_tensor(dt_[:, n, :], sum_sb[:, bass.ds(last_g, 1), :].rearrange("p o t -> p (o t)"),
                                           nzero[:, nn:nn + 1], psum[:, n, :], ALU.mult, ALU.add).then_inc(s_t, 1)

            def add_x1(g, half, n):
                e = (2 * g + half - 1) * 8 + n
                dve.wait_ge(s_du, e + 1)
                dve.wait_ge(s_x1l[n % 4], 16 * (2 * (2 * g + half - 1) + n // 4 + 1))
                v.tensor_tensor(dt_[:, n, :], dt_[:, n, :], x1r[:, n % 4, :], ALU.add).then_inc(s_o, 1)

            def half_group(g, half):
                for k in range(3):
                    y_low(g, half, k)
                zero_point(g, half)
                for k in range(3, NK):
                    y_low(g, half, k)
                    if 5 <= k < 13:
                        add_x1(g, half, k - 5)

            for k in range(NK):
                if 3 <= k + 2 < NK:
                    bits(k + 2)
                y_low(0, 0, k)
            half_group(0, 1)
            with dve.Fori(1, NG) as g:
                half_group(g, 0)
                half_group(g, 1)
            zero_point(NG, 0)
            for n in range(8):
                add_x1(NG, 0, n)


def kernel(x, itok_B_3_7, itok_B_0_7, itok_B_2182_4065, _lenS, L0_cond_A, L0_cond_B, L0_ffn_up, L0_ffn_down,
           L0_ffn_perm, L1_cond_W_sess, L1_cond_b_sess, L1_cond_W2, L1_cond_b2, L1_ffn_qweight,
           L1_ffn_weight_scale, L1_ffn_weight_zero_point, L1_ffn_bias):
    import concourse.bacc as bacc
    from concourse.bass_utils import run_bass_kernel_spmd

    def spread(a):
        a = np.asarray(a)
        return np.ascontiguousarray(np.broadcast_to(a[None, :], (P, a.shape[0])))

    def columns(a):
        return np.asarray(a).reshape(NK, P).T

    k = np.arange(D)
    word = 3 * (k // 4) + np.array([0, 0, 1, 2])[k % 4]
    p = np.arange(P)
    arrays = {
        "xT": np.asarray(x).reshape(NG, GT, D).transpose(0, 2, 1).reshape(NG * D, GT),
        "adown": np.asarray(L0_cond_A).transpose(1, 2, 0).reshape(D, R * NA),
        "bdown": np.asarray(L0_cond_B).transpose(2, 1, 0).reshape(D, R * NA),
        "up": np.asarray(L0_ffn_up).transpose(1, 0, 2).reshape(P, H * M),
        "down": np.asarray(L0_ffn_down).reshape(H, MT, P, P).transpose(2, 0, 1, 3).reshape(P, H * MT * P),
        "w_sess": np.asarray(L1_cond_W_sess).reshape(NS * C, HID),
        "b_sess": np.asarray(L1_cond_b_sess).reshape(NS, 2, P).transpose(2, 1, 0).reshape(P, 2 * NS),
        "w2": np.asarray(L1_cond_W2).reshape(2, P, P).transpose(1, 0, 2).reshape(P, 2 * P),
        "b2": np.asarray(L1_cond_b2).reshape(P, 1),
        "qw": np.asarray(L1_ffn_qweight).T[word],
        "dense": np.stack([columns(L1_ffn_weight_scale), columns(L1_ffn_weight_zero_point),
                           columns(L1_ffn_bias)], axis=1).reshape(P, 3 * NK),
        "perm": columns(L0_ffn_perm),
        "perm_row": spread(L0_ffn_perm),
        "adapter": spread(itok_B_3_7),
        "session": spread(itok_B_0_7),
        "chan_len": spread(_lenS),
        "time_len": spread(itok_B_2182_4065),
        "ident": np.eye(P, dtype=np.float32),
        "expand": (p[:, None] // NA == p[None, :] % R).astype(np.float32),
        "rows": np.stack([p, p % NA], axis=1).astype(np.float32),
    }
    arrays = {name: np.ascontiguousarray(a) for name, a in arrays.items()}
    nc = bacc.Bacc("TRN2", target_bir_lowering=False, num_devices=1)
    args = {name: nc.dram_tensor(name, a.shape, mybir.dt.from_np(a.dtype), kind="ExternalInput").ap()
            for name, a in arrays.items()}
    out = nc.dram_tensor("out", [NG * D, GT], F32, kind="ExternalOutput").ap()
    build(nc, **args, out=out)
    result = run_bass_kernel_spmd(nc, [arrays], core_ids=[0]).results[0]["out"]
    return result.reshape(NG, D, GT).transpose(0, 2, 1).reshape(B, C, D)
```
